# Optimizing a Trainium2 kernel written in Bass

```python
import numpy as np
import jax
import jax.numpy as jnp

def _softmax(x, axis=-1):
    return jax.nn.softmax(x, axis=axis)

def _gelu(x):
    return jax.nn.gelu(x, approximate=True)

def _silu(x):
    return jax.nn.silu(x)

def _sigmoid(x):
    return jax.nn.sigmoid(x)

def _layernorm(x, axis=-1, eps=1e-05):
    m = jnp.mean(x, axis=axis, keepdims=True)
    v = jnp.var(x, axis=axis, keepdims=True)
    return (x - m) / jnp.sqrt(v + eps)

def _scatter_add(tgt, idx, src, axis=0):
    return tgt.at[idx].add(src)

def _segment_sum(src, seg, n):
    return jax.ops.segment_sum(src, seg, n)
kernel_name = 'mk_gnn_preln_d2_gnn_r8_ef33e6'

def setup_inputs(seed: int=0):
    np.random.seed(seed)
    _w = jnp.asarray

    def _rec_inputs():
        import jax
        import jax.numpy as jnp
        _gk = jax.random.key(seed)
        x = -0.000202 + 1 * jax.random.normal(jax.random.fold_in(_gk, 1), (6250, 128), jnp.float32)
        _s = jax.random.randint(jax.random.fold_in(_gk, 2), (100000,), 0, 6250, jnp.int32)
        _d = jax.random.randint(jax.random.fold_in(_gk, 3), (100000,), 0, 6250, jnp.int32)
        _loop = jnp.arange(6250, dtype=jnp.int32)
        src = jnp.concatenate([_s, _d, _loop])
        dst = jnp.concatenate([_d, _s, _loop])
        _o = jnp.argsort(dst, stable=True)
        src = src[_o]
        dst = dst[_o]
        edge_weight = jax.random.uniform(jax.random.fold_in(_gk, 13), (206250,), jnp.float32, 0.0, 0.999998)
        return (x, src, dst, edge_weight)
    x, src, dst, edge_weight = _rec_inputs()

    def _L0_gnn_setup():
        import jax, jax.numpy as jnp
        import numpy as np
        N_NODES = 6250
        N_EDGES = 100000
        IN_FEAT = 128
        OUT_FEAT = 128
        key = jax.random.key(seed)
        ks = jax.random.split(key, 9)
        s = 1.0 / np.sqrt(IN_FEAT)
        return {'x': jax.random.normal(ks[0], (N_NODES, IN_FEAT), dtype=jnp.float32), 'src': jax.random.randint(ks[1], (N_EDGES,), 0, N_NODES), 'dst': jax.random.randint(ks[2], (N_EDGES,), 0, N_NODES), 'W1': jax.random.uniform(ks[3], (IN_FEAT, OUT_FEAT), jnp.float32, -s, s), 'b1': jax.random.uniform(ks[4], (OUT_FEAT,), jnp.float32, -s, s), 'W2': jax.random.uniform(ks[5], (OUT_FEAT, 1), jnp.float32, -s, s), 'b2': jax.random.uniform(ks[6], (1,), jnp.float32, -s, s), 'W4': jax.random.uniform(ks[7], (IN_FEAT, OUT_FEAT), jnp.float32, -s, s), 'b4': jax.random.uniform(ks[8], (OUT_FEAT,), jnp.float32, -s, s)}
    _L0_gnn_all = _L0_gnn_setup()
    _L0_gnn_in = {k: v for k, v in _L0_gnn_all.items() if k in ('W1', 'b1', 'W2', 'b2', 'W4', 'b4')}
    del _L0_gnn_all

    def _L1_gnn_setup():
        import jax, jax.numpy as jnp
        import numpy as np
        N_NODES = 6250
        N_EDGES = 75000
        GENE_DIM = 128
        HIDDEN = 128
        EPS = 1e-05

        def _gcn_conv(x, W, b, src, dst, ew):
            n = x.shape[0]
            h = x @ W
            loop = jnp.arange(n, dtype=src.dtype)
            s = jnp.concatenate([src, loop])
            d = jnp.concatenate([dst, loop])
            w = jnp.concatenate([ew, jnp.ones((n,), ew.dtype)])
            deg = jax.ops.segment_sum(w, d, num_segments=n)
            dinv = jax.lax.rsqrt(deg)
            norm = dinv[s] * w * dinv[d]
            out = jax.ops.segment_sum(h[s] * norm[:, None], d, num_segments=n)
            return out + b

        def _layer_norm(x, gamma, beta):
            mu = jnp.mean(x, axis=-1, keepdims=True)
            var = jnp.mean(jnp.square(x - mu), axis=-1, keepdims=True)
            return (x - mu) * jax.lax.rsqrt(var + EPS) * gamma + beta
        key = jax.random.key(seed)
        ks = jax.random.split(key, 12)
        glorot = lambda k, i, o: jax.random.normal(k, (i, o), jnp.float32) * np.sqrt(2.0 / (i + o)).astype(np.float32)
        return {'x': jax.random.normal(ks[0], (N_NODES, GENE_DIM), jnp.float32), 'edge_index': jax.random.randint(ks[1], (2, N_EDGES), 0, N_NODES, jnp.int64), 'edge_weight': jax.random.uniform(ks[2], (N_EDGES,), jnp.float32), 'W1': glorot(ks[3], GENE_DIM, HIDDEN), 'b1': jnp.zeros((HIDDEN,), jnp.float32), 'gamma1': jnp.ones((HIDDEN,), jnp.float32), 'beta1': jnp.zeros((HIDDEN,), jnp.float32), 'W2': glorot(ks[4], HIDDEN, HIDDEN), 'b2': jnp.zeros((HIDDEN,), jnp.float32), 'gamma2': jnp.ones((HIDDEN,), jnp.float32), 'beta2': jnp.zeros((HIDDEN,), jnp.float32)}
    _L1_gnn_all = _L1_gnn_setup()
    _L1_gnn_in = {k: v for k, v in _L1_gnn_all.items() if k in ('W1', 'b1', 'gamma1', 'beta1', 'W2', 'b2', 'gamma2', 'beta2')}
    del _L1_gnn_all
    return {'x': x, 'src': src, 'dst': dst, 'edge_weight': edge_weight, 'L0_gnn_W1': _L0_gnn_in['W1'], 'L0_gnn_b1': _L0_gnn_in['b1'], 'L0_gnn_W2': _L0_gnn_in['W2'], 'L0_gnn_b2': _L0_gnn_in['b2'], 'L0_gnn_W4': _L0_gnn_in['W4'], 'L0_gnn_b4': _L0_gnn_in['b4'], 'L1_gnn_W1': _L1_gnn_in['W1'], 'L1_gnn_b1': _L1_gnn_in['b1'], 'L1_gnn_gamma1': _L1_gnn_in['gamma1'], 'L1_gnn_beta1': _L1_gnn_in['beta1'], 'L1_gnn_W2': _L1_gnn_in['W2'], 'L1_gnn_b2': _L1_gnn_in['b2'], 'L1_gnn_gamma2': _L1_gnn_in['gamma2'], 'L1_gnn_beta2': _L1_gnn_in['beta2']}

def reference(x, src, dst, edge_weight, L0_gnn_W1, L0_gnn_b1, L0_gnn_W2, L0_gnn_b2, L0_gnn_W4, L0_gnn_b4, L1_gnn_W1, L1_gnn_b1, L1_gnn_gamma1, L1_gnn_beta1, L1_gnn_W2, L1_gnn_b2, L1_gnn_gamma2, L1_gnn_beta2):
    import jax
    import jax.numpy as jnp

    def _L0_gnn_ref(x, src, dst, W1, b1, W2, b2, W4, b4):
        import jax, jax.numpy as jnp
        import numpy as np
        N_NODES = 6250
        N_EDGES = 100000
        IN_FEAT = 128
        OUT_FEAT = 128
        n_nodes = x.shape[0]
        theta = x[dst] - x[src]
        w = jax.nn.sigmoid(jax.nn.relu(theta @ W1 + b1) @ W2 + b2)
        w_theta = w * theta
        agg = jax.ops.segment_sum(w_theta, dst, num_segments=n_nodes)
        indeg = jax.ops.segment_sum(jnp.ones((dst.shape[0], 1), x.dtype), dst, num_segments=n_nodes)
        return agg + indeg * (x @ W4 + b4)

    def _L1_gnn_ref(x, edge_index, edge_weight, W1, b1, gamma1, beta1, W2, b2, gamma2, beta2):
        import jax, jax.numpy as jnp
        import numpy as np
        N_NODES = 6250
        N_EDGES = 75000
        GENE_DIM = 128
        HIDDEN = 128
        EPS = 1e-05

        def _gcn_conv(x, W, b, src, dst, ew):
            n = x.shape[0]
            h = x @ W
            loop = jnp.arange(n, dtype=src.dtype)
            s = jnp.concatenate([src, loop])
            d = jnp.concatenate([dst, loop])
            w = jnp.concatenate([ew, jnp.ones((n,), ew.dtype)])
            deg = jax.ops.segment_sum(w, d, num_segments=n)
            dinv = jax.lax.rsqrt(deg)
            norm = dinv[s] * w * dinv[d]
            out = jax.ops.segment_sum(h[s] * norm[:, None], d, num_segments=n)
            return out + b

        def _layer_norm(x, gamma, beta):
            mu = jnp.mean(x, axis=-1, keepdims=True)
            var = jnp.mean(jnp.square(x - mu), axis=-1, keepdims=True)
            return (x - mu) * jax.lax.rsqrt(var + EPS) * gamma + beta
        src, dst = (edge_index[0], edge_index[1])
        h = _gcn_conv(x, W1, b1, src, dst, edge_weight)
        h = jax.nn.relu(_layer_norm(h, gamma1, beta1))
        h = _gcn_conv(h, W2, b2, src, dst, edge_weight)
        h = _layer_norm(h, gamma2, beta2)
        return h
    edge_index = jnp.stack([src, dst])
    h = jnp.maximum(_layernorm(x, axis=-1), 0.0)
    x = x + _L0_gnn_ref(h, src, dst, L0_gnn_W1, L0_gnn_b1, L0_gnn_W2, L0_gnn_b2, L0_gnn_W4, L0_gnn_b4)
    h = jnp.maximum(_layernorm(x, axis=-1), 0.0)
    x = x + _L1_gnn_ref(h, edge_index, edge_weight, L1_gnn_W1, L1_gnn_b1, L1_gnn_gamma1, L1_gnn_beta1, L1_gnn_W2, L1_gnn_b2, L1_gnn_gamma2, L1_gnn_beta2)
    return x

_drawn_inputs = setup_inputs


def setup_inputs(seed=0):
    import zlib

    import numpy as np

    out = dict(_drawn_inputs(seed))
    spreads = {'L1_gnn_b1': (0.0, 0.662),
     'L1_gnn_gamma1': (1.0, 0.6),
     'L1_gnn_beta1': (0.0, 2.0),
     'L1_gnn_b2': (0.0, 0.8),
     'L1_gnn_gamma2': (1.0, 0.6),
     'L1_gnn_beta2': (0.0, 0.8)}
    factors = {'edge_weight': 64.0, 'L0_gnn_b1': 25.9}
    for name, (base, spread) in spreads.items():
        noise = np.random.default_rng([zlib.crc32(name.encode()), seed]).standard_normal(out[name].shape)
        drawn = base * np.exp(spread * noise) if base else spread * noise
        out[name] = jnp.asarray(drawn.astype(out[name].dtype))
    for name, factor in factors.items():
        out[name] = (out[name] * factor).astype(out[name].dtype)
    return out
```

```python
from contextlib import ExitStack

import concourse.bass as bass
from concourse import mybir

F32, BF16, I32 = mybir.dt.float32, mybir.dt.bfloat16, mybir.dt.int32
ALU = mybir.AluOpType
ACT = mybir.ActivationFunctionType
AX = mybir.AxisListType

N = 6250
F = 128
E = 206250
P = 128
EPS = 1e-5

K = 8
GE = K * P
NG = -(-E // GE)
NG += NG % 2
NIT = NG // 2
NGP = NG + 2
EP = NGP * GE
GPP = 2
GROWS = NGP // GPP
U = 2
KU = K // U

TB = 4
NB = -(-(N + P) // (TB * P))
NT = NB * TB
NP = NT * P

C_W, C_ONE, C_EW = F, F + 1, F + 2
AW = F + 3
NCH = NG * K


def ds(start, size):
    return bass.ds(start, size)


def build_program(nc, x, src, dst, ew, c, out):
    table0 = nc.dram_tensor("table0", (NP, 2 * F), F32).ap()
    pwin_d = nc.dram_tensor("pwin_d", (NP, 3 * F), BF16).ap()
    table1 = nc.dram_tensor("table1", (NP, F), F32).ap()
    table2 = nc.dram_tensor("table2", (NP, F), F32).ap()
    sums0 = nc.dram_tensor("sums0", (NP, AW), F32).ap()
    sums1 = nc.dram_tensor("sums1", (NP, F), F32).ap()
    sums2 = nc.dram_tensor("sums2", (NP, F), F32).ap()
    relp_d = nc.dram_tensor("relp_d", (EP,), F32).ap()
    relr_d = nc.dram_tensor("relr_d", (EP,), BF16).ap()
    base_d = nc.dram_tensor("base_d", (NGP,), F32).ap()

    ctx = ExitStack()
    with ctx:
        def sb(name, shape, dt=F32):
            return ctx.enter_context(nc.sbuf_tensor(name, shape, dt))

        def pb(name, shape, dt=F32):
            return ctx.enter_context(nc.psum_tensor(name, shape, dt))

        def sem(name):
            return ctx.enter_context(nc.semaphore(name))

        X = sb("X", [P, NT, F])
        A = sb("A", [P, NT, AW])
        H = sb("H", [P, NT, F])
        Q = sb("Q", [P, NT, F])
        G = sb("G", [P, NT, F])
        mv = sb("mv", [P, NT, 2])
        rstd = sb("rstd", [P, NT])
        nmr = sb("nmr", [P, NT])
        dinv = sb("dinv", [P, NT])
        g_i32 = G[:, :, :].rearrange("p t f -> p (t f)").bitcast(I32)
        h_f32 = H[:, :, :].rearrange("p t f -> p (t f)")
        SP_E = GPP * GE
        dst_i = g_i32[0:GROWS, 0:SP_E]
        nxt_i = g_i32[0:GROWS, SP_E:2 * SP_E]
        gap = G[:, :, :].rearrange("p t f -> p (t f)")[0:GROWS, 2 * SP_E:3 * SP_E]
        relp_all = h_f32[0:GROWS, 0:SP_E]
        relr_all = h_f32[0:GROWS, SP_E:SP_E + SP_E // 2].bitcast(BF16)
        zeros = h_f32[:, 4096:4096 + (NT // 4) * AW]

        ident = sb("ident", [P, P])
        iota_row = sb("iota_row", [P, P])
        iota_col = sb("iota_col", [P, 1])
        iota_dif = sb("iota_dif", [P, P])
        below = sb("below", [P, P])
        ones_row = sb("ones_row", [1, P])
        W14 = sb("W14", [P, 2 * F])
        WG = [sb("WG1", [P, F]), sb("WG2", [P, F])]
        vec = {n: sb("v_" + n, [P, F]) for n in ("b1", "w2", "b4", "c1", "gm1", "bt1", "c2", "gm2", "bt2")}
        b2col = sb("b2col", [P, 1])
        basef = sb("basef", [GROWS, GPP])
        span = sb("span", [GROWS, GPP])
        small = sb("small", [GROWS, 4])
        bad = sb("bad", [P, 1])
        badmax = sb("badmax", [1, 1])
        flag = sb("flag", [1, 1], I32)
        base_row = sb("base_row", [1, NGP])
        delta_row = sb("delta_row", [1, NGP])
        delta = sb("delta", [P, NGP])
        stats = sb("stats", [P, TB, 6])
        mvb = sb("mvb", [P, TB, 2])
        stage = sb("stage", [P, TB, F])
        hT = sb("hT", [P, TB, P])
        tst = sb("tst", [P, TB, 2 * F])
        pw3 = sb("pw3", [P, TB, 3 * F], BF16)
        idx = [sb(f"idx{b}", [P, K], I32) for b in range(2)]
        relp = [sb(f"relp{b}", [P, K]) for b in range(2)]
        relr = [sb(f"relr{b}", [P, GE], BF16) for b in range(2)]
        eww = [sb(f"eww{b}", [P, K]) for b in range(2)]
        pwin = [sb(f"pwin{b}", [P, 3 * F], BF16) for b in range(2)]
        rows = [sb(f"rows{u}", [P, KU, 2 * F]) for u in range(2 * U)]
        ohT = [sb(f"ohT{b}", [P, K, P], BF16) for b in range(2)]
        oh = [sb(f"oh{b}", [P, K, P]) for b in range(2)]
        eqm = sb("eqm", [P, K, P])
        shift = [sb(f"shift{b}", [P, P]) for b in range(2)]
        diff = sb("diff", [P, KU, F])
        gated = sb("gated", [P, KU, F])
        z = [sb(f"z{h}", [P, KU]) for h in range(U)]
        V = [sb(f"V{b}", [P, K, AW]) for b in range(2)]
        R = [sb(f"R{b}", [P, AW]) for b in range(2)]
        pb1, pres = gated, diff
        tmpa, tmpb, tmpc = eqm[:, 0:TB, :], eqm[:, TB:2 * TB, :], diff
        g_dst = idx[1][:, 0:1]
        g_src = idx[0][:, 0:1]
        g_put = idx[1][:, 1:2]
        g_ew = eww[0][:, 0:1]
        g_dstf = eww[0][:, 1:2]
        g_cnt = eww[0][:, 2:3]
        g_dup = eww[0][:, 3:4]
        g_z = eww[0][:, 4:5]
        g_row = eqm[:, 0, :].bitcast(I32)
        g_eq = oh[0][:, 0, :]
        g_low = oh[0][:, 1, :]
        g_from = rows[0][:, 0, :]
        g_to = rows[1][:, 0, :]
        g_acc = R[0]
        g_new = R[1]
        g_v = V[0][:, 0, :]

        psE = [pb(f"psE{h}", [P, KU, P]) for h in range(U)]
        psA = [pb(f"psA{b}", [P, 512]) for b in range(2)]
        psT = pb("psT", [P, TB, P])
        psO = pb("psO", [P, TB, 2 * F])

        ld_edge = sem("ld_edge")
        ld_x = sem("ld_x")
        ld_const = sem("ld_const")
        ld_h = sem("ld_h")
        iotas = sem("iotas")
        passed = sem("passed")
        ident_ready = sem("ident_ready")
        pro = sem("pro")
        bad_T = sem("bad_T")
        flag_ready = sem("flag_ready")
        base_ready = sem("base_ready")
        base_back = sem("base_back")
        delta_mm = sem("delta_mm")
        delta_ready = sem("delta_ready")
        rel_made = sem("rel_made")
        rel_stored = sem("rel_stored")
        zeros_ready = sem("zeros_ready")
        zeroed = sem("zeroed")
        tables_ready = [sem(f"tables_ready{n}") for n in range(3)]
        pass_done = [sem(f"pass_done{n}") for n in range(3)]
        sums_back = [sem(f"sums_back{n}") for n in range(3)]
        out_stored = sem("out_stored")
        scaled = sem("scaled")

        def node_sems(tag, names):
            return {n: sem(f"{n}_{tag}") for n in names.split()}

        common = "own own2 stat sd rs norm "
        turned = "stage_ready tr_done hT_ready mm_done out_done row_stored "
        nodes = [
            node_sems("a", common + turned + "p_copied h_copied pw_made win_stored"),
            node_sems("b", common + turned + "made add cq"),
            node_sems("c", common + turned + "made"),
            node_sems("d", common + "made"),
        ]

        def pass_sems(n):
            pairs = "idx_ready rel_ready oh_ready acc_done R_ready stored "
            pairs += "pwin_ready ohT_ready psE_ready psE_free z_ready" if n == 0 else "eq"
            s = {name: [sem(f"{name}{n}_{b}") for b in range(2)] for name in pairs.split()}
            s["rows_ready"] = [sem(f"rows_ready{n}_{u}") for u in range(2 * U)]
            s["rows_used"] = [sem(f"rows_used{n}_{u}") for u in range(2 * U)]
            if n == 0:
                s["gated"], s["sig"] = sem("gated0"), sem("sig0")
                s["g_z"], s["g_w"] = s["gated"], s["sig"]
            s["g_nodes"], s["g_edges"] = s["rel_ready"]
            s["g_rows"], s["g_sums"], s["g_put"] = s["rows_ready"][0:3]
            s["g_v"], s["g_new"], s["g_free"] = s["rows_used"][0:3]
            s["g_own"], s["g_mm"] = s["oh_ready"]
            return s

        passes = [pass_sems(n) for n in range(3)]
        tables = [table0, table1, table2]
        sums = [sums0, sums1, sums2]
        widths = [AW, F, F]

        def blk(t, i):
            return t[:, ds(i * TB, TB), :]

        def per_node(t, i):
            return t[:, ds(i * TB, TB)].unsqueeze(2).broadcast_to([P, TB, F])

        def per_feature(v):
            return v[:, :].unsqueeze(1).broadcast_to([P, TB, F])

        def rows_of(t, i):
            return t[ds(i * (TB * P), TB * P), :].rearrange("(t p) f -> p t f", p=P)

        def all_rows(t):
            return t.rearrange("(t p) f -> p t f", p=P)

        def wait_apart(e, *waits):
            for semaphore, value in waits:
                e.wait_ge(semaphore, value)
            e.sem_inc(passed, 1)

        def is_windowed(e):
            e.wait_ge(flag_ready, 1)
            return e.value_load(flag[0:1, 0:1], min_val=0, max_val=1) > 0

        block = ctx.enter_context(nc.Block())

        @block.sync
        def _(sp):
            two = lambda a: a.rearrange("(g e) -> g e", e=GPP * GE)
            sp.dma_start(dst_i, two(dst[0:EP])).then_inc(ld_edge, 16)
            sp.dma_start(nxt_i, two(dst[1:EP + 1])).then_inc(ld_edge, 16)
            sp.dma_start(X[:, :, :], all_rows(x)).then_inc(ld_x, 16)
            sp.wait_ge(zeros_ready, 1)
            for n in range(3):
                quarter = NP // 4
                for q in range(4):
                    part = sums[n][q * quarter:(q + 1) * quarter, :].rearrange("(p r) c -> p (r c)", p=P)
                    sp.dma_start(part, zeros[:, 0:NT // 4 * widths[n]]).then_inc(zeroed, 16)
            sp.wait_ge(base_ready, 1)
            sp.dma_start(base_d.rearrange("(g e) -> g e", e=GPP), basef[:, :]).then_inc(base_back, 16)
            sp.wait_ge(base_back, 16)
            sp.dma_start(base_row[:, :], base_d.rearrange("(a g) -> a g", a=1)).then_inc(base_back, 16)
            sp.wait_ge(rel_made, 1)
            sp.dma_start(two(relp_d), relp_all).then_inc(rel_stored, 16)
            sp.dma_start(two(relr_d), relr_all).then_inc(rel_stored, 16)

            s = nodes[0]
            with sp.Fori(0, NB) as i:
                wait_apart(sp, (s["p_copied"], i + 2))
                wait_apart(sp, (s["h_copied"], i + 2))
                sp.dma_start(rows_of(table0, i), tst[:, :, :]).then_inc(s["row_stored"], 16)
                sp.wait_ge(s["pw_made"], i + 1)
                sp.dma_start(rows_of(pwin_d, i), pw3[:, :, :]).then_inc(s["win_stored"], 16)
            sp.wait_ge(s["row_stored"], 16 * (NB + 1))
            sp.wait_ge(s["win_stored"], 16 * (NB + 1))
            sp.wait_ge(rel_stored, 32)
            sp.wait_ge(zeroed, 16 * 12)
            sp.sem_inc(tables_ready[0], 1)
            sp.dma_start(H[:, :, :], all_rows(table0)[:, :, F:2 * F]).then_inc(ld_h, 16)

            windowed = is_windowed(sp)
            for n in range(3):
                s = passes[n]
                last_iter = NIT
                if n:
                    sp.wait_ge(tables_ready[n], 1)

                def load_group(g, b):
                    part = lambda a: a[ds(g * GE, GE)]
                    sp.dma_start(relp[b][:, :], part(relp_d).rearrange("(p j) -> p j", j=K)).then_inc(s["rel_ready"][b], 16)
                    sp.dma_start(eww[b][:, :], part(ew).rearrange("(p j) -> p j", j=K)).then_inc(s["rel_ready"][b], 16)
                    if n == 0:
                        sp.dma_start(relr[b][:, :], part(relr_d).partition_broadcast(P)).then_inc(s["rel_ready"][b], 16)
                        first = sp.value_load(dst[ds(g * GE, 1)].rearrange("(a b) -> a b", a=1), min_val=0, max_val=N)
                        sp.dma_start(pwin[b][:, :], pwin_d[ds(first, P), :]).then_inc(s["pwin_ready"][b], 16)

                def load_idx(g, b):
                    sp.dma_start(idx[b][:, :], src[ds(g * GE, GE)].rearrange("(p j) -> p j", j=K)).then_inc(s["idx_ready"][b], 16)

                with sp.If(windowed):
                    load_idx(0, 0)
                    load_idx(1, 1)
                    load_group(0, 0)
                    with sp.Fori(0, NIT) as i:
                        for b in range(2):
                            sp.wait_ge(s["acc_done"][1 - b], i + 1 + b)
                            load_group(2 * i + (b + 1), 1 - b)
                            for u in (U * b, U * b + 1):
                                sp.wait_ge(s["rows_ready"][u], (i + 1) * 16 * KU)
                            load_idx(2 * i + (b + 2), b)
                    sp.wait_ge(s["rel_ready"][0], 16 * (3 if n == 0 else 2) * (NIT + 1))
                    if n == 0:
                        sp.wait_ge(s["pwin_ready"][0], 16 * (NIT + 1))
                    for b in range(2):
                        sp.wait_ge(s["idx_ready"][b], 16 * (NIT + 1))
                with sp.Else():
                    with sp.Fori(0, NCH) as k:
                        sp.wait_ge(s["g_free"], k + 1)
                        part = lambda a: a[ds(k * P, P)].rearrange("(p a) -> p a", a=1)
                        sp.dma_start(g_src, part(src)).then_inc(s["g_nodes"], 16)
                        sp.dma_start(g_dst, part(dst)).then_inc(s["g_nodes"], 16)
                        sp.dma_start(g_ew, part(ew)).then_inc(s["g_edges"], 16)
                        sp.dma_start(g_row, dst[ds(k * P, P)].partition_broadcast(P)).then_inc(s["g_edges"], 16)

                sp.wait_ge(pass_done[n], 1)
                sp.dma_start(A[:, :, 0:widths[n]], all_rows(sums[n])).then_inc(sums_back[n], 16)
                if n < 2:
                    s = nodes[n + 1]
                    with sp.Fori(0, NB) as i:
                        sp.wait_ge(s["made"], i + 1)
                        sp.dma_start(rows_of(tables[n + 1], i), blk(G, i)).then_inc(s["row_stored"], 16)
                    sp.wait_ge(s["row_stored"], 16 * NB)
                    sp.sem_inc(tables_ready[n + 1], 1)
            s = nodes[3]
            full = N // (TB * P)
            with sp.Fori(0, full) as i:
                sp.wait_ge(s["made"], i + 1)
                sp.dma_start(rows_of(out, i), blk(H, i)).then_inc(out_stored, 16)
            sp.wait_ge(s["made"], NB)
            t0 = full * TB
            stores = full
            while t0 * P < N:
                r = min(P, N - t0 * P)
                sp.dma_start(out[t0 * P:t0 * P + r, :], H[0:r, t0, :]).then_inc(out_stored, 16)
                t0 += 1
                stores += 1
            sp.wait_ge(out_stored, 16 * stores)

        @block.gpsimd
        def _(pool):
            small_ok = dict(allow_small_or_imprecise_dtypes=True)
            pool.iota(iota_row[:, :], pattern=[[1, P]], base=0, channel_multiplier=0, **small_ok).then_inc(iotas, 1)
            pool.iota(iota_col[:, :], pattern=[[0, 1]], base=0, channel_multiplier=1, **small_ok).then_inc(iotas, 1)
            pool.iota(iota_dif[:, :], pattern=[[-1, P]], base=0, channel_multiplier=1, **small_ok).then_inc(iotas, 1)

            s = nodes[0]
            pool.sem_inc(s["h_copied"], 1)
            with pool.Fori(0, NB) as i:
                wait_apart(pool, (s["stage_ready"], i + 1), (s["row_stored"], 16 * i + 16))
                pool.tensor_copy(tst[:, :, F:2 * F], stage[:, :, :]).then_inc(s["h_copied"], 1)

            windowed = is_windowed(pool)
            for n in range(3):
                s = passes[n]
                width = 2 * F if n == 0 else F
                pool.wait_ge(tables_ready[n], 1)
                with pool.If(windowed):
                    with pool.Fori(0, NIT) as i:
                        for b in range(2):
                            for h in range(U):
                                u = U * b + h
                                wait_apart(pool, (s["idx_ready"][b], (i + 1) * 16), (s["rows_used"][u], i + 1))
                                for j in range(KU):
                                    pool.indirect_dma_start(
                                        out=rows[u][:, j, 0:width], out_offset=None, in_=tables[n],
                                        in_offset=bass.IndirectOffsetOnAxis(ap=idx[b][:, h * KU + j:h * KU + j + 1], axis=0),
                                    ).then_inc(s["rows_ready"][u], 16)
                with pool.Else():
                    with pool.Fori(0, NCH) as k:
                        wait_apart(pool, (s["g_nodes"], (k + 1) * 32))
                        pool.indirect_dma_start(
                            out=g_from[:, 0:width], out_offset=None, in_=tables[n],
                            in_offset=bass.IndirectOffsetOnAxis(ap=g_src, axis=0)).then_inc(s["g_rows"], 16)
                        if n == 0:
                            pool.indirect_dma_start(
                                out=g_to, out_offset=None, in_=tables[n],
                                in_offset=bass.IndirectOffsetOnAxis(ap=g_dst, axis=0)).then_inc(s["g_rows"], 16)
                        pool.indirect_dma_start(
                            out=g_acc[:, 0:widths[n]], out_offset=None, in_=sums[n],
                            in_offset=bass.IndirectOffsetOnAxis(ap=g_dst, axis=0)).then_inc(s["g_sums"], 16)
                        wait_apart(pool, (s["g_new"], k + 1))
                        pool.indirect_dma_start(
                            out=sums[n], out_offset=bass.IndirectOffsetOnAxis(ap=g_put, axis=0),
                            in_=g_new[:, 0:widths[n]], in_offset=None,
                            bounds_check=NP - 1, oob_is_err=False).then_inc(s["g_put"], 16)
                        wait_apart(pool, (s["g_put"], (k + 1) * 16))
                        pool.sem_inc(s["g_free"], 1)
                    pool.sem_inc(pass_done[n], 1)
                if n == 0:
                    s = nodes[1]
                    pool.wait_ge(sums_back[0], 16)
                    with pool.Fori(0, NB) as i:
                        cnt = A[:, ds(i * TB, TB), C_ONE:C_ONE + 1].broadcast_to([P, TB, F])
                        pool.tensor_tensor(blk(Q, i), blk(Q, i), cnt, ALU.mult).then_inc(s["cq"], 1)

        @block.scalar
        def _(act):
            act.dma_start(ident[:, :], c["identity"]).then_inc(ident_ready, 16)
            act.dma_start(W14[:, 0:F], c["L0_gnn_W1"]).then_inc(ld_const, 16)
            act.dma_start(W14[:, F:2 * F], c["L0_gnn_W4"]).then_inc(ld_const, 16)
            act.dma_start(WG[0][:, :], c["L1_gnn_W1"]).then_inc(ld_const, 16)
            act.dma_start(WG[1][:, :], c["L1_gnn_W2"]).then_inc(ld_const, 16)
            act.dma_start(vec["w2"][:, :], c["L0_gnn_W2"].rearrange("f a -> (f a)").partition_broadcast(P)).then_inc(ld_const, 16)
            act.dma_start(b2col[:, :], c["L0_gnn_b2"].partition_broadcast(P)).then_inc(ld_const, 16)
            for v, name in (("b1", "L0_gnn_b1"), ("b4", "L0_gnn_b4"), ("c1", "L1_gnn_b1"), ("gm1", "L1_gnn_gamma1"),
                            ("bt1", "L1_gnn_beta1"), ("c2", "L1_gnn_b2"), ("gm2", "L1_gnn_gamma2"), ("bt2", "L1_gnn_beta2")):
                act.dma_start(vec[v][:, :], c[name].partition_broadcast(P)).then_inc(ld_const, 16)
            act.wait_ge(ld_const, 16 * 14)

            def transform(s, from_x, width):
                act.sem_inc(s["hT_ready"], 1)
                if width == 2 * F:
                    act.sem_inc(s["p_copied"], 1)
                src_rows = X if from_x else H
                with act.Fori(0, NB) as i:
                    if from_x:
                        act.wait_ge(s["tr_done"], i + 1)
                        if width == 2 * F:
                            act.wait_ge(s["h_copied"], i + 1)
                        for t in range(TB):
                            at = ds(i * TB + t, 1)
                            done = act.activation(stage[:, t, :], src_rows[:, at, :].rearrange("p a f -> p (a f)"),
                                                  ACT.Relu, bias=nmr[:, at], scale=rstd[:, at])
                        done.then_inc(s["stage_ready"], 1)
                    act.wait_ge(s["tr_done"], i + 2)
                    act.wait_ge(s["mm_done"], i + 1)
                    act.activation(hT[:, :, :], psT[:, :, :], ACT.Copy).then_inc(s["hT_ready"], 1)
                    if width == 2 * F:
                        act.wait_ge(s["out_done"], i + 2)
                        act.wait_ge(s["row_stored"], 16 * i + 16)
                        act.activation(tst[:, :, 0:F], psO[:, :, 0:F], ACT.Copy).then_inc(s["p_copied"], 1)

            def std(s):
                act.wait_ge(s["stat"], 1)
                act.activation(rstd[:, :], rstd[:, :], ACT.Sqrt).then_inc(s["sd"], 1)
                act.wait_ge(s["rs"], 1)

            std(nodes[0])
            transform(nodes[0], True, 2 * F)

            windowed = is_windowed(act)
            for n in range(3):
                s = passes[n]
                w = widths[n]
                with act.If(windowed):
                    act.wait_ge(tables_ready[n], 1)
                    for b in range(2):
                        act.sem_inc(s["stored"][b], 16)
                    if n == 0:
                        for u in range(2 * U):
                            act.sem_inc(s["rows_used"][u], 1)
                        act.sem_inc(s["sig"], 2)
                    with act.Fori(0, NIT) as i:
                        for b in range(2):
                            g = 2 * i + b
                            first = act.value_load(dst[ds(g * GE, 1)].rearrange("(a b) -> a b", a=1), min_val=0, max_val=N)
                            if n == 0:
                                act.wait_ge(s["acc_done"][b], i + 1)
                                act.wait_ge(s["oh_ready"][b], i + 2)
                                for h in range(U):
                                    u = U * b + h
                                    act.wait_ge(s["z_ready"][h], 2 * i + (b + 1))
                                    act.activation(V[b][:, h * KU:(h + 1) * KU, C_W:C_W + 1], z[h][:, :].unsqueeze(2),
                                                   ACT.Sigmoid, bias=b2col[:, 0:1]).then_inc(s["sig"], 1)
                                    act.wait_ge(s["sig"], 4 * i + (2 * b + h + 3))
                                    for j in range(KU):
                                        jj = h * KU + j
                                        done = act.activation(V[b][:, jj, 0:F], rows[u][:, j, F:2 * F], ACT.Copy,
                                                              scale=V[b][:, jj, C_W:C_W + 1])
                                    done.then_inc(s["rows_used"][u], 1)
                            act.wait_ge(s["acc_done"][b], i + 2)
                            act.wait_ge(s["stored"][b], (i + 1) * 16)
                            act.activation(R[b][:, 0:w], psA[b][:, 0:w], ACT.Copy).then_inc(s["R_ready"][b], 1)
                            act.wait_ge(s["R_ready"][b], i + 2)
                            act.wait_ge(s["stored"][1 - b], (i + 1 + b) * 16)
                            act.dma_start(sums[n][ds(first, P), :], R[b][:, 0:w]).then_inc(s["stored"][b], 16)
                    for b in range(2):
                        act.wait_ge(s["stored"][b], 16 * (NIT + 1))
                    act.sem_inc(pass_done[n], 1)
                with act.Else():
                    if n == 0:
                        with act.Fori(0, NCH) as k:
                            act.wait_ge(s["g_z"], k + 1)
                            act.activation(g_v[:, C_W:C_W + 1], g_z, ACT.Sigmoid, bias=b2col[:, 0:1]).then_inc(s["g_w"], 1)
                s = nodes[n + 1]
                if n == 0:
                    act.wait_ge(s["add"], 1)
                    act.activation(dinv[:, :], dinv[:, :], ACT.Sqrt).then_inc(scaled, 1)
                std(s)
                if n == 0:
                    transform(s, True, F)
                elif n == 1:
                    transform(s, False, F)

        @block.tensor
        def _(pe):
            pe.wait_ge(ident_ready, 16)
            pe.wait_ge(pro, 8)
            pe.transpose(psT[0:1, 0, :], bad[:, :], ident[:, :]).then_inc(bad_T, 1)
            pe.wait_ge(delta_ready, 1)
            pe.matmul(psA[0][:, 0:NGP], ones_row[:, :], delta_row[:, :], start=True, stop=True).then_inc(delta_mm, 1)
            pe.wait_ge(ld_const, 16 * 14)
            pe.wait_ge(flag_ready, 1)

            def transform(s, weight, width):
                pe.sem_inc(s["tr_done"], 1)
                pe.sem_inc(s["mm_done"], 1)
                with pe.Fori(0, NB) as i:
                    pe.wait_ge(s["stage_ready"], i + 1)
                    pe.wait_ge(s["hT_ready"], i + 1)
                    for t in range(TB):
                        done = pe.transpose(psT[:, t, :], stage[:, t, :], ident[:, :])
                    done.then_inc(s["tr_done"], 1)
                    pe.wait_ge(s["hT_ready"], i + 2)
                    pe.wait_ge(s["out_done"], i + 1)
                    if width == 2 * F:
                        pe.wait_ge(s["p_copied"], i + 1)
                    for t in range(TB):
                        done = pe.matmul(psO[:, t, 0:width], hT[:, t, :], weight[:, :], start=True, stop=True)
                    done.then_inc(s["mm_done"], 1)

            transform(nodes[0], W14, 2 * F)

            windowed = is_windowed(pe)
            for n in range(3):
                s = passes[n]
                w = widths[n]
                with pe.If(windowed):
                    for b in range(2):
                        pe.sem_inc(s["acc_done"][b], 1)
                    if n:
                        for u in range(2 * U):
                            pe.sem_inc(s["rows_used"][u], 1)
                    with pe.Fori(0, NIT) as i:
                        for b in range(2):
                            if n == 0:
                                pe.wait_ge(s["ohT_ready"][b], i + 1)
                                pe.wait_ge(s["pwin_ready"][b], (i + 1) * 16)
                                for h in range(U):
                                    pe.wait_ge(s["psE_free"][h], 2 * i + (b + 1))
                                    for j in range(KU):
                                        for part in range(3):
                                            done = pe.matmul(psE[h][:, j, :], ohT[b][:, h * KU + j, :],
                                                             pwin[b][:, part * F:(part + 1) * F],
                                                             start=(part == 0), stop=(part == 2))
                                    done.then_inc(s["psE_ready"][h], 1)
                            pe.wait_ge(s["oh_ready"][b], i + 2)
                            pe.wait_ge(s["R_ready"][b], i + 1)
                            for h in range(U):
                                u = U * b + h
                                if n == 0:
                                    pe.wait_ge(s["rows_used"][u], i + 2)
                                else:
                                    pe.wait_ge(s["rows_ready"][u], (i + 1) * 16 * KU)
                                for j in range(KU):
                                    jj = h * KU + j
                                    value = V[b][:, jj, 0:w] if n == 0 else rows[u][:, j, 0:F]
                                    done = pe.matmul(psA[b][:, 0:w], oh[b][:, jj, :], value, start=(jj == 0), stop=False)
                                if n:
                                    done.then_inc(s["rows_used"][u], 1)
                            pe.wait_ge(s["R_ready"][1 - b], i + 1 + b)
                            pe.matmul(psA[b][:, 0:w], shift[b][:, :], R[1 - b][:, 0:w], start=False, stop=True)\
                              .then_inc(s["acc_done"][b], 1)
                with pe.Else():
                    with pe.Fori(0, NCH) as k:
                        pe.wait_ge(s["g_v"], k + 1)
                        pe.matmul(psA[0][:, 0:w], g_eq, g_v[:, 0:w], start=True, stop=True).then_inc(s["g_mm"], 1)
                if n < 2:
                    transform(nodes[n + 1], WG[n], F)

        @block.vector
        def _(dve):
            dve.memset(zeros, 0.0).then_inc(zeros_ready, 1)
            dve.memset(ones_row[:, :], 1.0)
            dve.memset(bad[:, :], -1.0)
            for b in range(2):
                dve.memset(V[b][:, :, C_ONE:C_ONE + 1], 1.0)
            dve.wait_ge(iotas, 3)
            dve.tensor_scalar(below[:, :], iota_dif[:, :], 0.0, None, ALU.is_gt)

            by_group = lambda a: a.rearrange("r (g e) -> r g e", g=GPP)
            dve.wait_ge(ld_edge, 32)
            dve.tensor_copy(basef[:, :].unsqueeze(2), by_group(dst_i)[:, :, 0:1]).then_inc(pro, 1)
            dve.tensor_tensor(gap, nxt_i, dst_i, ALU.subtract).then_inc(pro, 1)
            dve.wait_ge(pro, 1)
            dve.sem_inc(base_ready, 1)
            dve.tensor_tensor(span[:, :].unsqueeze(2), by_group(dst_i)[:, :, GE - 1:GE], basef[:, :].unsqueeze(2),
                              ALU.subtract).then_inc(pro, 1)
            dve.wait_ge(pro, 3)
            dve.tensor_reduce(small[:, 0:1], gap, AX.X, ALU.min).then_inc(pro, 1)
            dve.tensor_reduce(small[:, 1:2], span[:, :], AX.X, ALU.max).then_inc(pro, 1)
            dve.wait_ge(pro, 5)
            dve.tensor_scalar(small[:, 2:3], small[:, 1:2], float(1 - P), None, ALU.add).then_inc(pro, 1)
            dve.tensor_scalar(small[:, 3:4], small[:, 0:1], -1.0, None, ALU.mult).then_inc(pro, 1)
            dve.wait_ge(pro, 7)
            dve.tensor_tensor(bad[0:GROWS, :], small[:, 2:3], small[:, 3:4], ALU.max).then_inc(pro, 1)
            for q in range(GPP):
                dve.tensor_scalar(by_group(relp_all)[:, q, :], by_group(dst_i)[:, q, :], basef[:, q:q + 1], None, ALU.subtract)
                by_chunk = by_group(relr_all)[:, q, :].rearrange("r (j p) -> r p j", j=K)
                done = dve.tensor_scalar(by_chunk, by_group(dst_i)[:, q, :].rearrange("r (p j) -> r p j", j=K),
                                         basef[:, q:q + 1], None, ALU.subtract)
            done.then_inc(rel_made, 1)
            dve.wait_ge(bad_T, 1)
            dve.tensor_reduce(badmax[:, :], psT[0:1, 0, :], AX.X, ALU.max).then_inc(pro, 1)
            dve.wait_ge(pro, 9)
            dve.tensor_scalar(flag[:, :], badmax[:, :], 0.0, None, ALU.is_le).then_inc(flag_ready, 1)
            dve.memset(delta_row[:, 0:1], 0.0)
            dve.wait_ge(base_back, 32)
            dve.tensor_tensor(delta_row[:, 1:NGP], base_row[:, 1:NGP], base_row[:, 0:NGP - 1], ALU.subtract)\
               .then_inc(delta_ready, 1)
            dve.wait_ge(delta_mm, 1)
            dve.tensor_copy(delta[:, :], psA[0][:, 0:NGP]).then_inc(pro, 1)
            dve.wait_ge(pro, 10)
            dve.wait_ge(ld_const, 16 * 14)

            def block_stats(s, i, t):
                for q in range(TB):
                    done = dve.bn_stats(stats[:, q, :], t[:, ds(i * TB + q, 1), :].rearrange("p a f -> p (a f)"))
                done.then_inc(s["own2"], 1)
                wait_apart(dve, (s["own2"], 3 * i + 1))
                for q in range(TB):
                    done = dve.bn_aggr(mvb[:, q, :], stats[:, q, :])
                done.then_inc(s["own2"], 1)
                dve.wait_ge(s["own2"], 3 * i + 2)
                dve.tensor_copy(blk(mv, i), mvb[:, :, :]).then_inc(s["own2"], 1)

            def finish_stats(s):
                dve.wait_ge(s["own2"], 3 * NB)
                dve.tensor_scalar(rstd[:, :].unsqueeze(2), mv[:, :, 1:2], EPS, None, ALU.add).then_inc(s["stat"], 1)
                dve.wait_ge(s["sd"], 1)
                dve.reciprocal(rstd[:, :], rstd[:, :]).then_inc(s["norm"], 1)
                dve.wait_ge(s["norm"], 1)
                dve.scalar_tensor_tensor(nmr[:, :].unsqueeze(2), mv[:, :, 0:1], -1.0, rstd[:, :].unsqueeze(2),
                                         ALU.mult, ALU.mult).then_inc(s["rs"], 1)

            s = nodes[0]
            dve.wait_ge(ld_x, 16)
            with dve.Fori(0, NB) as i:
                block_stats(s, i, X)
            finish_stats(s)
            dve.sem_inc(s["out_done"], 1)
            dve.sem_inc(s["row_stored"], 16)
            dve.sem_inc(s["win_stored"], 16)
            with dve.Fori(0, NB) as i:
                dve.wait_ge(s["mm_done"], i + 2)
                dve.tensor_tensor(pb1[:, :, :], psO[:, :, 0:F], per_feature(vec["b1"]), ALU.add).then_inc(s["own"], 1)
                dve.tensor_tensor(blk(Q, i), psO[:, :, F:2 * F], per_feature(vec["b4"]), ALU.add).then_inc(s["out_done"], 1)
                dve.wait_ge(s["own"], 4 * i + 1)
                dve.wait_ge(s["win_stored"], 16 * i + 16)
                dve.tensor_copy(pw3[:, :, 0:F], pb1[:, :, :]).then_inc(s["own"], 1)
                dve.wait_ge(s["own"], 4 * i + 2)
                dve.tensor_tensor(pres[:, :, :], pb1[:, :, :], pw3[:, :, 0:F], ALU.subtract).then_inc(s["own"], 1)
                dve.wait_ge(s["own"], 4 * i + 3)
                dve.tensor_copy(pw3[:, :, F:2 * F], pres[:, :, :]).then_inc(s["own"], 1)
                dve.wait_ge(s["own"], 4 * i + 4)
                dve.tensor_tensor(pw3[:, :, 2 * F:3 * F], pres[:, :, :], pw3[:, :, F:2 * F], ALU.subtract)\
                   .then_inc(s["pw_made"], 1)

            windowed = is_windowed(dve)
            for n in range(3):
                s = passes[n]
                w = widths[n]
                with dve.If(windowed):
                    dve.memset(R[1][:, :], 0.0).then_inc(s["R_ready"][1], 1)
                    dve.sem_inc(s["R_ready"][0], 1)
                    for b in range(2):
                        dve.sem_inc(s["oh_ready"][b], 1)
                        if n == 0:
                            dve.sem_inc(s["psE_free"][b], 1)
                    with dve.Fori(0, NIT) as i:
                        for b in range(2):
                            per_group = 3 if n == 0 else 2
                            dve.wait_ge(s["rel_ready"][b], (i + 1) * (16 * per_group))
                            if n == 0:
                                dve.tensor_scalar(ohT[b][:, :, :], relr[b][:, :].rearrange("p (j e) -> p j e", j=K),
                                                  iota_col[:, 0:1], None, ALU.is_equal).then_inc(s["ohT_ready"][b], 1)
                            dve.wait_ge(s["acc_done"][b], i + 1)
                            node = iota_row[:, :].unsqueeze(1).broadcast_to([P, K, P])
                            rel = relp[b][:, :].unsqueeze(2).broadcast_to([P, K, P])
                            dve.tensor_scalar(shift[b][:, :], iota_dif[:, :], delta[:, ds(2 * i + b, 1)], None, ALU.is_equal)
                            if n == 0:
                                dve.tensor_copy(V[b][:, :, C_EW:C_EW + 1], eww[b][:, :].unsqueeze(2))
                                dve.tensor_tensor(oh[b][:, :, :], node, rel, ALU.is_equal).then_inc(s["oh_ready"][b], 1)
                            else:
                                dve.wait_ge(s["oh_ready"][1 - b], i + (1 + b))
                                dve.tensor_tensor(eqm[:, :, :], node, rel, ALU.is_equal).then_inc(s["eq"][b], 1)
                                dve.wait_ge(s["eq"][b], i + 1)
                                dve.tensor_tensor(oh[b][:, :, :], eqm[:, :, :], eww[b][:, :].unsqueeze(2).broadcast_to([P, K, P]),
                                                  ALU.mult).then_inc(s["oh_ready"][b], 1)
                            if n == 0:
                                for h in range(U):
                                    u = U * b + h
                                    dve.wait_ge(s["psE_ready"][h], 2 * i + (b + 1))
                                    dve.wait_ge(s["rows_ready"][u], (i + 1) * 16 * KU)
                                    dve.tensor_tensor(diff[:, :, :], psE[h][:, :, :], rows[u][:, :, 0:F], ALU.subtract)\
                                       .then_inc(s["psE_free"][h], 1)
                                    dve.wait_ge(s["psE_free"][h], 2 * i + (b + 2))
                                    dve.scalar_tensor_tensor(gated[:, :, :], diff[:, :, :], 0.0, per_feature(vec["w2"]),
                                                             ALU.max, ALU.mult).then_inc(s["gated"], 1)
                                    dve.wait_ge(s["gated"], 4 * i + (2 * b + h + 1))
                                    dve.wait_ge(s["sig"], 4 * i + (2 * b + h + 1))
                                    dve.tensor_reduce(z[h][:, :], gated[:, :, :], AX.X, ALU.add).then_inc(s["z_ready"][h], 1)
                with dve.Else():
                    OWN = 8 if n == 0 else 4
                    gathers = 2 if n == 0 else 1
                    dve.sem_inc(s["g_free"], 1)
                    with dve.Fori(0, NCH) as k:
                        own = lambda m: dve.wait_ge(s["g_own"], k * OWN + m)
                        dve.wait_ge(s["g_nodes"], (k + 1) * 32)
                        dve.wait_ge(s["g_edges"], (k + 1) * 32)
                        dve.tensor_copy(g_dstf, g_dst).then_inc(s["g_own"], 1)
                        own(1)
                        dve.tensor_scalar(g_eq, g_row, g_dstf, None, ALU.is_equal).then_inc(s["g_own"], 1)
                        own(2)
                        dve.tensor_tensor(g_low, g_eq, below[:, :], ALU.mult).then_inc(s["g_own"], 1)
                        own(3)
                        dve.tensor_reduce(g_cnt, g_low, AX.X, ALU.max).then_inc(s["g_own"], 1)
                        own(4)
                        dve.scalar_tensor_tensor(g_put, g_cnt, float(2 * NP), g_dstf, ALU.mult, ALU.add)
                        dve.wait_ge(s["g_rows"], (k + 1) * (16 * gathers))
                        if n == 0:
                            dve.tensor_tensor(diff[:, 0, :], g_to[:, 0:F], g_from[:, 0:F], ALU.subtract).then_inc(s["g_own"], 1)
                            own(5)
                            dve.tensor_tensor(diff[:, 1, :], diff[:, 0, :], vec["b1"][:, :], ALU.add).then_inc(s["g_own"], 1)
                            own(6)
                            dve.scalar_tensor_tensor(gated[:, 0, :], diff[:, 1, :], 0.0, vec["w2"][:, :], ALU.max, ALU.mult)\
                               .then_inc(s["g_own"], 1)
                            own(7)
                            dve.tensor_reduce(g_z, gated[:, 0, :], AX.X, ALU.add).then_inc(s["g_z"], 1)
                            dve.tensor_copy(g_v[:, C_EW:C_EW + 1], g_ew).then_inc(s["g_own"], 1)
                            dve.wait_ge(s["g_w"], k + 1)
                            own(8)
                            dve.tensor_scalar(g_v[:, 0:F], g_from[:, F:2 * F], g_v[:, C_W:C_W + 1], None, ALU.mult)\
                               .then_inc(s["g_v"], 1)
                        else:
                            dve.tensor_scalar(g_v[:, 0:F], g_from[:, 0:F], g_ew, None, ALU.mult).then_inc(s["g_v"], 1)
                        dve.wait_ge(s["g_mm"], k + 1)
                        dve.wait_ge(s["g_sums"], (k + 1) * 16)
                        dve.tensor_tensor(g_new[:, 0:w], psA[0][:, 0:w], g_acc[:, 0:w], ALU.add).then_inc(s["g_new"], 1)

                s = nodes[n + 1]
                dve.wait_ge(sums_back[n], 16)
                if n == 0:
                    dve.tensor_scalar(dinv[:, :].unsqueeze(2), A[:, :, C_EW:C_EW + 1], 1.0, None, ALU.add).then_inc(s["add"], 1)
                    dve.wait_ge(ld_h, 16)
                    with dve.Fori(0, NB) as i:
                        sw = A[:, ds(i * TB, TB), C_W:C_W + 1].broadcast_to([P, TB, F])
                        swh = A[:, ds(i * TB, TB), 0:F]
                        dve.tensor_tensor(tmpa[:, :, :], blk(H, i), sw, ALU.mult).then_inc(s["own"], 1)
                        dve.wait_ge(s["own"], 4 * i + 1)
                        dve.tensor_tensor(tmpb[:, :, :], tmpa[:, :, :], swh, ALU.subtract).then_inc(s["own"], 1)
                        dve.wait_ge(s["own"], 4 * i + 2)
                        dve.wait_ge(s["cq"], i + 1)
                        dve.tensor_tensor(tmpc[:, :, :], tmpb[:, :, :], blk(Q, i), ALU.add).then_inc(s["own"], 1)
                        dve.wait_ge(s["own"], 4 * i + 3)
                        dve.tensor_tensor(blk(X, i), blk(X, i), tmpc[:, :, :], ALU.add).then_inc(s["own"], 1)
                        wait_apart(dve, (s["own"], 4 * i + 4))
                        block_stats(s, i, X)
                    dve.wait_ge(scaled, 1)
                    dve.reciprocal(dinv[:, :], dinv[:, :]).then_inc(s["norm"], 1)
                    dve.wait_ge(s["own2"], 3 * NB)
                    dve.tensor_scalar(rstd[:, :].unsqueeze(2), mv[:, :, 1:2], EPS, None, ALU.add).then_inc(s["stat"], 1)
                    dve.wait_ge(s["sd"], 1)
                    dve.reciprocal(rstd[:, :], rstd[:, :]).then_inc(s["norm"], 1)
                    dve.wait_ge(s["norm"], 2)
                    dve.scalar_tensor_tensor(nmr[:, :].unsqueeze(2), mv[:, :, 0:1], -1.0, rstd[:, :].unsqueeze(2),
                                             ALU.mult, ALU.mult).then_inc(s["rs"], 1)
                else:
                    bias, gamma, beta = (vec[v + str(n)] for v in ("c", "gm", "bt"))
                    with dve.Fori(0, NB) as i:
                        dve.tensor_tensor(tmpa[:, :, :], A[:, ds(i * TB, TB), 0:F], blk(G, i), ALU.add).then_inc(s["own"], 1)
                        dve.wait_ge(s["own"], 3 * i + 1)
                        dve.tensor_tensor(tmpb[:, :, :], tmpa[:, :, :], per_node(dinv, i), ALU.mult).then_inc(s["own"], 1)
                        dve.wait_ge(s["own"], 3 * i + 2)
                        dve.tensor_tensor(blk(H, i), tmpb[:, :, :], per_feature(bias), ALU.add).then_inc(s["own"], 1)
                        wait_apart(dve, (s["own"], 3 * i + 3))
                        block_stats(s, i, H)
                    finish_stats(s)

                def normed(i, steps, base):
                    for q in range(TB):
                        at = ds(i * TB + q, 1)
                        done = dve.tensor_scalar(tmpa[:, q, :], H[:, at, :].rearrange("p a f -> p (a f)"),
                                                 rstd[:, at], nmr[:, at], ALU.mult, ALU.add)
                    done.then_inc(s["norm"], 1)
                    dve.wait_ge(s["norm"], steps * i + (base + 1))
                    dve.tensor_tensor(tmpc[:, :, :], tmpa[:, :, :], per_feature(gamma), ALU.mult).then_inc(s["norm"], 1)
                    dve.wait_ge(s["norm"], steps * i + (base + 2))
                    dve.tensor_tensor(tmpb[:, :, :], tmpc[:, :, :], per_feature(beta), ALU.add).then_inc(s["norm"], 1)
                    dve.wait_ge(s["norm"], steps * i + (base + 3))

                if n < 2:
                    dve.wait_ge(s["rs"], 1)
                    dve.sem_inc(s["out_done"], 1)
                    with dve.Fori(0, NB) as i:
                        if n == 1:
                            normed(i, 3, 1)
                            dve.wait_ge(s["tr_done"], i + 1)
                            dve.tensor_scalar(stage[:, :, :], tmpb[:, :, :], 0.0, None, ALU.max).then_inc(s["stage_ready"], 1)
                        dve.wait_ge(s["mm_done"], i + 2)
                        dve.tensor_tensor(blk(G, i), psO[:, :, 0:F], per_node(dinv, i), ALU.mult).then_inc(s["out_done"], 1)
                        dve.wait_ge(s["out_done"], i + 2)
                        dve.sem_inc(s["made"], 1)
                else:
                    dve.wait_ge(s["rs"], 1)
                    with dve.Fori(0, NB) as i:
                        normed(i, 3, 1)
                        dve.tensor_tensor(blk(H, i), tmpb[:, :, :], blk(X, i), ALU.add).then_inc(s["made"], 1)


_WEIGHTS = ["L0_gnn_W1", "L0_gnn_b1", "L0_gnn_W2", "L0_gnn_b2", "L0_gnn_W4", "L0_gnn_b4", "L1_gnn_W1", "L1_gnn_b1",
            "L1_gnn_gamma1", "L1_gnn_beta1", "L1_gnn_W2", "L1_gnn_b2", "L1_gnn_gamma2", "L1_gnn_beta2"]


def kernel(**inputs):
    import numpy as np
    import concourse.bacc as bacc
    from concourse.bass_utils import run_bass_kernel_spmd

    def padded(a, n, value):
        out = np.full((n,) + a.shape[1:], value, a.dtype)
        out[:a.shape[0]] = a
        return out

    arrays = {
        "x": padded(np.asarray(inputs["x"]), NP, 0),
        "src": padded(np.asarray(inputs["src"]), EP, 0),
        "dst": padded(np.asarray(inputs["dst"]), EP + 1, N),
        "edge_weight": padded(np.asarray(inputs["edge_weight"]), EP, 0),
        "identity": np.eye(P, dtype=np.float32),
    }
    for name in _WEIGHTS:
        arrays[name] = np.ascontiguousarray(inputs[name])

    nc = bacc.Bacc("TRN2", target_bir_lowering=False, num_devices=1)
    args = {}
    for name, a in arrays.items():
        args[name] = nc.dram_tensor(f"in_{name}", a.shape, mybir.dt.from_np(a.dtype), kind="ExternalInput").ap()
    out = nc.dram_tensor("out_x", (N, F), F32, kind="ExternalOutput").ap()
    build_program(nc, args["x"], args["src"], args["dst"], args["edge_weight"], args, out)
    r = run_bass_kernel_spmd(nc, [{f"in_{k}": v for k, v in arrays.items()}], core_ids=[0])
    return r.results[0]["out_x"]
```

```python
from contextlib import ExitStack

import concourse.bass as bass
from concourse import mybir

F32, BF16, I32 = mybir.dt.float32, mybir.dt.bfloat16, mybir.dt.int32
ALU = mybir.AluOpType
ACT = mybir.ActivationFunctionType
AX = mybir.AxisListType

N = 6250
F = 128
E = 206250
P = 128
EPS = 1e-5

K = 8
GE = K * P
NG = -(-E // GE)
NG += NG % 2
NIT = NG // 2
NGP = NG + 2
EP = NGP * GE
GPP = 2
GROWS = NGP // GPP
U = 2
KU = K // U

TB = 4
NB = -(-(N + P) // (TB * P))
NT = NB * TB
NP = NT * P

PARTS = [(0, 4), (4, 7), (7, 10), (10, NB)]

C_W, C_ONE, C_EW = F, F + 1, F + 2
AW = F + 3
NCH = NG * K


def ds(start, size):
    return bass.ds(start, size)


def build_program(nc, x, src, dst, ew, c, out):
    table0 = nc.dram_tensor("table0", (NP, 2 * F), F32).ap()
    pwin_d = nc.dram_tensor("pwin_d", (NP, 3 * F), BF16).ap()
    table1 = nc.dram_tensor("table1", (NP, F), F32).ap()
    table2 = nc.dram_tensor("table2", (NP, F), F32).ap()
    sums0 = nc.dram_tensor("sums0", (NP, AW), F32).ap()
    sums1 = nc.dram_tensor("sums1", (NP, F), F32).ap()
    sums2 = nc.dram_tensor("sums2", (NP, F), F32).ap()
    relp_d = nc.dram_tensor("relp_d", (EP,), F32).ap()
    relr_d = nc.dram_tensor("relr_d", (EP,), BF16).ap()
    base_d = nc.dram_tensor("base_d", (NGP,), F32).ap()

    ctx = ExitStack()
    with ctx:
        def sb(name, shape, dt=F32):
            return ctx.enter_context(nc.sbuf_tensor(name, shape, dt))

        def pb(name, shape, dt=F32):
            return ctx.enter_context(nc.psum_tensor(name, shape, dt))

        def sem(name):
            return ctx.enter_context(nc.semaphore(name))

        X = sb("X", [P, NT, F])
        A = sb("A", [P, NT, AW])
        H = sb("H", [P, NT, F])
        Q = sb("Q", [P, NT, F])
        G = sb("G", [P, NT, F])
        mv = sb("mv", [P, NT, 2])
        rstd = sb("rstd", [P, NT])
        nmr = sb("nmr", [P, NT])
        dinv = sb("dinv", [P, NT])
        g_i32 = G[:, :, :].rearrange("p t f -> p (t f)").bitcast(I32)
        h_f32 = H[:, :, :].rearrange("p t f -> p (t f)")
        SP_E = GPP * GE
        dst_i = g_i32[0:GROWS, 0:SP_E]
        nxt_i = g_i32[0:GROWS, SP_E:2 * SP_E]
        gap = G[:, :, :].rearrange("p t f -> p (t f)")[0:GROWS, 2 * SP_E:3 * SP_E]
        relp_all = h_f32[0:GROWS, 0:SP_E]
        relr_all = h_f32[0:GROWS, SP_E:SP_E + SP_E // 2].bitcast(BF16)
        zeros = h_f32[:, 4096:4096 + (NT // 4) * AW]

        ident = sb("ident", [P, P])
        iota_row = sb("iota_row", [P, P])
        iota_col = sb("iota_col", [P, 1])
        iota_dif = sb("iota_dif", [P, P])
        below = sb("below", [P, P])
        ones_row = sb("ones_row", [1, P])
        W14 = sb("W14", [P, 2 * F])
        WG = [sb("WG1", [P, F]), sb("WG2", [P, F])]
        vec = {n: sb("v_" + n, [P, F]) for n in ("b1", "w2", "b4", "c1", "gm1", "bt1", "c2", "gm2", "bt2")}
        b2col = sb("b2col", [P, 1])
        basef = sb("basef", [GROWS, GPP])
        span = sb("span", [GROWS, GPP])
        small = sb("small", [GROWS, 4])
        bad = sb("bad", [P, 1])
        badmax = sb("badmax", [1, 1])
        flag = sb("flag", [1, 1], I32)
        base_row = sb("base_row", [1, NGP])
        first_i = sb("first_i", [1, NGP], I32)
        delta_row = sb("delta_row", [1, NGP])
        delta = sb("delta", [P, NGP])
        stats = sb("stats", [P, TB, 6])
        mvb = sb("mvb", [P, TB, 2])
        stage = sb("stage", [P, TB, F])
        hT = sb("hT", [P, TB, P])
        tst = sb("tst", [P, TB, 2 * F])
        pw3 = sb("pw3", [P, TB, 3 * F], BF16)
        idx = [sb(f"idx{b}", [P, K], I32) for b in range(2)]
        relp = [sb(f"relp{b}", [P, K]) for b in range(2)]
        relr = [sb(f"relr{b}", [P, GE], BF16) for b in range(2)]
        eww = [sb(f"eww{b}", [P, K]) for b in range(2)]
        pwin = [sb(f"pwin{b}", [P, 3 * F], BF16) for b in range(2)]
        rows = [sb(f"rows{u}", [P, KU, 2 * F]) for u in range(2 * U)]
        ohT = [sb(f"ohT{b}", [P, K, P], BF16) for b in range(2)]
        oh = [sb(f"oh{b}", [P, K, P]) for b in range(2)]
        eqm = sb("eqm", [P, K, P])
        shift = [sb(f"shift{b}", [P, P]) for b in range(2)]
        diff = sb("diff", [P, KU, F])
        gated = sb("gated", [P, KU, F])
        z = [sb(f"z{h}", [P, KU]) for h in range(U)]
        V = [sb(f"V{b}", [P, K, AW]) for b in range(2)]
        R = [sb(f"R{b}", [P, AW]) for b in range(2)]
        pres = diff
        tmpa, tmpb, tmpc = eqm[:, 0:TB, :], eqm[:, TB:2 * TB, :], diff
        g_dst = idx[1][:, 0:1]
        g_src = idx[0][:, 0:1]
        g_put = idx[1][:, 1:2]
        g_ew = eww[0][:, 0:1]
        g_dstf = eww[0][:, 1:2]
        g_cnt = eww[0][:, 2:3]
        g_dup = eww[0][:, 3:4]
        g_z = eww[0][:, 4:5]
        g_row = eqm[:, 0, :].bitcast(I32)
        g_eq = oh[0][:, 0, :]
        g_low = oh[0][:, 1, :]
        g_from = rows[0][:, 0, :]
        g_to = rows[1][:, 0, :]
        g_acc = R[0]
        g_new = R[1]
        g_v = V[0][:, 0, :]

        psE = [pb(f"psE{h}", [P, KU, P]) for h in range(U)]
        psA = [pb(f"psA{b}", [P, 512]) for b in range(2)]
        psT = pb("psT", [P, TB, P])
        psO = pb("psO", [P, TB, 2 * F])

        ld_edge = sem("ld_edge")
        ld_x = sem("ld_x")
        ld_const = sem("ld_const")
        ld_h = sem("ld_h")
        iotas = sem("iotas")
        passed = sem("passed")
        ident_ready = sem("ident_ready")
        pro = sem("pro")
        bad_T = sem("bad_T")
        flag_ready = sem("flag_ready")
        base_ready = sem("base_ready")
        base_back = sem("base_back")
        delta_mm = sem("delta_mm")
        delta_ready = sem("delta_ready")
        rel_made = sem("rel_made")
        rel_stored = sem("rel_stored")
        zeros_ready = sem("zeros_ready")
        zeroed = sem("zeroed")
        tables_ready = [sem(f"tables_ready{n}") for n in range(3)]
        pass_done = [sem(f"pass_done{n}") for n in range(3)]
        sums_back = [sem(f"sums_back{part}") for part in range(len(PARTS))]
        out_stored = sem("out_stored")
        scaled = sem("scaled")

        def node_sems(tag, names):
            return {n: sem(f"{n}_{tag}") for n in names.split()}

        common = "own own2 "
        turned = "stage_ready tr_done hT_ready mm_done out_done row_stored "
        nodes = [
            node_sems("a", common + turned + "p_made h_copied pw_made win_stored"),
            node_sems("b", common + turned + "add added half"),
            node_sems("c", common + turned + "added normed"),
            node_sems("d", common + "made added normed"),
        ]

        stat, sd, norm, rs = sem("stat"), sem("sd"), sem("norm"), sem("rs")

        def pass_sems(n):
            pairs = "idx_ready rel_ready oh_ready acc_done R_ready stored "
            pairs += "pwin_ready ohT_ready psE_ready psE_free z_ready" if n == 0 else "eq"
            s = {name: [sem(f"{name}{n}_{b}") for b in range(2)] for name in pairs.split()}
            s["rows_ready"] = [sem(f"rows_ready{n}_{u}") for u in range(2 * U)]
            s["rows_used"] = [sem(f"rows_used{n}_{u}") for u in range(2 * U)]
            if n == 0:
                s["gated"], s["sig"] = sem("gated0"), sem("sig0")
                s["g_z"], s["g_w"] = s["gated"], s["sig"]
            s["g_nodes"], s["g_edges"] = s["rel_ready"]
            s["g_rows"], s["g_sums"], s["g_put"] = s["rows_ready"][0:3]
            s["g_v"], s["g_new"], s["g_free"] = s["rows_used"][0:3]
            s["g_own"], s["g_mm"] = s["oh_ready"]
            return s

        passes = [pass_sems(n) for n in range(3)]
        tables = [table0, table1, table2]
        sums = [sums0, sums1, sums2]
        widths = [AW, F, F]

        def blk(t, i):
            return t[:, ds(i * TB, TB), :]

        def per_node(t, i):
            return t[:, ds(i * TB, TB)].unsqueeze(2).broadcast_to([P, TB, F])

        def per_feature(v):
            return v[:, :].unsqueeze(1).broadcast_to([P, TB, F])

        def rows_of(t, i):
            return t[ds(i * (TB * P), TB * P), :].rearrange("(t p) f -> p t f", p=P)

        def by_group(t):
            return t.rearrange("r (g e) -> r g e", g=GPP)

        def tile_of(t, i, q):
            return t[:, ds(i * TB + q, 1), 0:F].rearrange("p a f -> p (a f)")

        def all_rows(t):
            return t.rearrange("(t p) f -> p t f", p=P)

        def wait_apart(e, *waits):
            for semaphore, value in waits:
                e.wait_ge(semaphore, value)
            e.sem_inc(passed, 1)

        def is_windowed(e):
            e.wait_ge(flag_ready, 1)
            return e.value_load(flag[0:1, 0:1], min_val=0, max_val=1) > 0

        def first_node(e, g):
            return e.value_load(first_i[:, ds(g, 1)], min_val=0, max_val=N)

        block = ctx.enter_context(nc.Block())

        @block.sync
        def _(sp):
            two = lambda a: a.rearrange("(g e) -> g e", e=GPP * GE)
            sp.dma_start(dst_i, two(dst[0:EP])).then_inc(ld_edge, 16)
            sp.dma_start(nxt_i, two(dst[1:EP + 1])).then_inc(ld_edge, 16)
            sp.dma_start(X[:, :, :], all_rows(x)).then_inc(ld_x, 16)
            sp.wait_ge(zeros_ready, 1)
            for n in range(3):
                quarter = NP // 4
                for q in range(4):
                    part = sums[n][q * quarter:(q + 1) * quarter, :].rearrange("(p r) c -> p (r c)", p=P)
                    sp.dma_start(part, zeros[:, 0:NT // 4 * widths[n]]).then_inc(zeroed, 16)
            sp.wait_ge(base_ready, 1)
            sp.dma_start(base_d.rearrange("(g e) -> g e", e=GPP), basef[:, :]).then_inc(base_back, 16)
            sp.wait_ge(base_back, 16)
            sp.dma_start(base_row[:, :], base_d.rearrange("(a g) -> a g", a=1)).then_inc(base_back, 16)
            sp.wait_ge(rel_made, GPP)
            sp.dma_start(two(relp_d), relp_all).then_inc(rel_stored, 16)
            sp.dma_start(two(relr_d), relr_all).then_inc(rel_stored, 16)

            s = nodes[0]
            with sp.Fori(0, NB) as i:
                wait_apart(sp, (s["p_made"], i + 1))
                wait_apart(sp, (s["h_copied"], i + 2))
                sp.dma_start(rows_of(table0, i), tst[:, :, :]).then_inc(s["row_stored"], 16)
                sp.wait_ge(s["pw_made"], i + 1)
                sp.dma_start(rows_of(pwin_d, i), pw3[:, :, :]).then_inc(s["win_stored"], 16)
            sp.wait_ge(s["row_stored"], 16 * (NB + 1))
            sp.wait_ge(s["win_stored"], 16 * (NB + 1))
            sp.wait_ge(rel_stored, 32)
            sp.wait_ge(zeroed, 16 * 12)
            sp.sem_inc(tables_ready[0], 1)
            sp.dma_start(H[:, :, :], all_rows(table0)[:, :, F:2 * F]).then_inc(ld_h, 16)

            windowed = is_windowed(sp)
            for n in range(3):
                s = passes[n]
                if n:
                    sp.wait_ge(tables_ready[n], 1)

                def load_idx(g, b):
                    sp.dma_start(idx[b][:, :], src[ds(g * GE, GE)].rearrange("(p j) -> p j", j=K)).then_inc(s["idx_ready"][b], 16)

                def load_rel(g, b):
                    part = lambda a: a[ds(g * GE, GE)]
                    if n == 0:
                        sp.dma_start(relr[b][:, :], part(relr_d).partition_broadcast(P)).then_inc(s["rel_ready"][b], 16)
                    sp.dma_start(relp[b][:, :], part(relp_d).rearrange("(p j) -> p j", j=K)).then_inc(s["rel_ready"][b], 16)
                    sp.dma_start(eww[b][:, :], part(ew).rearrange("(p j) -> p j", j=K)).then_inc(s["rel_ready"][b], 16)

                def load_pwin(first, b):
                    sp.dma_start(pwin[b][:, :], pwin_d[ds(first, P), :]).then_inc(s["pwin_ready"][b], 16)

                with sp.If(windowed):
                    for b in range(2):
                        load_idx(b, b)
                        load_rel(b, b)
                        if n == 0:
                            load_pwin(first_node(sp, b), b)
                    with sp.Fori(0, NIT) as i:
                        for b in range(2):
                            g = 2 * i + (b + 2)
                            for u in (U * b, U * b + 1):
                                sp.wait_ge(s["rows_ready"][u], (i + 1) * 16 * KU)
                            load_idx(g, b)
                            wait_apart(sp, (s["oh_ready"][b], i + 2))
                            load_rel(g, b)
                            if n == 0:
                                first = first_node(sp, g)
                                wait_apart(sp, (s["psE_free"][1], 2 * i + (b + 2)))
                                load_pwin(first, b)
                    for b in range(2):
                        sp.wait_ge(s["idx_ready"][b], 16 * (NIT + 1))
                        sp.wait_ge(s["rel_ready"][b], 16 * (3 if n == 0 else 2) * (NIT + 1))
                        if n == 0:
                            sp.wait_ge(s["pwin_ready"][b], 16 * (NIT + 1))
                with sp.Else():
                    with sp.Fori(0, NCH) as k:
                        sp.wait_ge(s["g_free"], k + 1)
                        part = lambda a: a[ds(k * P, P)].rearrange("(p a) -> p a", a=1)
                        sp.dma_start(g_src, part(src)).then_inc(s["g_nodes"], 16)
                        sp.dma_start(g_dst, part(dst)).then_inc(s["g_nodes"], 16)
                        sp.dma_start(g_ew, part(ew)).then_inc(s["g_edges"], 16)
                        sp.dma_start(g_row, dst[ds(k * P, P)].partition_broadcast(P)).then_inc(s["g_edges"], 16)

                sp.wait_ge(pass_done[n], 1)
                for part, (lo, hi) in enumerate(PARTS):
                    at = slice(lo * TB, hi * TB)
                    sp.dma_start(A[:, at, 0:widths[n]], all_rows(sums[n])[:, at, :]).then_inc(sums_back[part], 16)
                if n < 2:
                    s = nodes[n + 1]
                    with sp.Fori(0, NB) as i:
                        sp.wait_ge(s["out_done"], i + 2)
                        sp.dma_start(rows_of(tables[n + 1], i), blk(G, i)).then_inc(s["row_stored"], 16)
                    sp.wait_ge(s["row_stored"], 16 * NB)
                    sp.sem_inc(tables_ready[n + 1], 1)
            s = nodes[3]
            full = N // (TB * P)
            with sp.Fori(0, full) as i:
                sp.wait_ge(s["made"], i + 1)
                sp.dma_start(rows_of(out, i), blk(H, i)).then_inc(out_stored, 16)
            sp.wait_ge(s["made"], NB)
            t0 = full * TB
            stores = full
            while t0 * P < N:
                r = min(P, N - t0 * P)
                sp.dma_start(out[t0 * P:t0 * P + r, :], H[0:r, t0, :]).then_inc(out_stored, 16)
                t0 += 1
                stores += 1
            sp.wait_ge(out_stored, 16 * stores)

        @block.gpsimd
        def _(pool):
            small_ok = dict(allow_small_or_imprecise_dtypes=True)
            pool.iota(iota_row[:, :], pattern=[[1, P]], base=0, channel_multiplier=0, **small_ok).then_inc(iotas, 1)
            pool.iota(iota_col[:, :], pattern=[[0, 1]], base=0, channel_multiplier=1, **small_ok).then_inc(iotas, 1)
            pool.iota(iota_dif[:, :], pattern=[[-1, P]], base=0, channel_multiplier=1, **small_ok).then_inc(iotas, 1)

            pool.wait_ge(ld_edge, 32)
            pool.wait_ge(pro, 1)
            for q in range(GPP):
                pool.tensor_scalar(by_group(relp_all)[:, q, :], by_group(dst_i)[:, q, :], basef[:, q:q + 1], None,
                                   ALU.subtract)
                pool.tensor_scalar(by_group(relr_all)[:, q, :].rearrange("r (j p) -> r p j", j=K),
                                   by_group(dst_i)[:, q, :].rearrange("r (p j) -> r p j", j=K),
                                   basef[:, q:q + 1], None, ALU.subtract).then_inc(rel_made, 1)

            s = nodes[0]
            pool.sem_inc(s["h_copied"], 1)
            with pool.Fori(0, NB) as i:
                wait_apart(pool, (s["stage_ready"], i + 1), (s["row_stored"], 16 * i + 16))
                pool.tensor_copy(tst[:, :, F:2 * F], stage[:, :, :]).then_inc(s["h_copied"], 1)

            windowed = is_windowed(pool)
            for n in range(3):
                s = passes[n]
                width = 2 * F if n == 0 else F
                pool.wait_ge(tables_ready[n], 1)
                with pool.If(windowed):
                    with pool.Fori(0, NIT) as i:
                        for b in range(2):
                            for h in range(U):
                                u = U * b + h
                                wait_apart(pool, (s["idx_ready"][b], (i + 1) * 16), (s["rows_used"][u], i + 1))
                                for j in range(KU):
                                    pool.indirect_dma_start(
                                        out=rows[u][:, j, 0:width], out_offset=None, in_=tables[n],
                                        in_offset=bass.IndirectOffsetOnAxis(ap=idx[b][:, h * KU + j:h * KU + j + 1], axis=0),
                                    ).then_inc(s["rows_ready"][u], 16)
                with pool.Else():
                    with pool.Fori(0, NCH) as k:
                        wait_apart(pool, (s["g_nodes"], (k + 1) * 32))
                        pool.indirect_dma_start(
                            out=g_from[:, 0:width], out_offset=None, in_=tables[n],
                            in_offset=bass.IndirectOffsetOnAxis(ap=g_src, axis=0)).then_inc(s["g_rows"], 16)
                        if n == 0:
                            pool.indirect_dma_start(
                                out=g_to, out_offset=None, in_=tables[n],
                                in_offset=bass.IndirectOffsetOnAxis(ap=g_dst, axis=0)).then_inc(s["g_rows"], 16)
                        pool.indirect_dma_start(
                            out=g_acc[:, 0:widths[n]], out_offset=None, in_=sums[n],
                            in_offset=bass.IndirectOffsetOnAxis(ap=g_dst, axis=0)).then_inc(s["g_sums"], 16)
                        wait_apart(pool, (s["g_new"], k + 1))
                        pool.indirect_dma_start(
                            out=sums[n], out_offset=bass.IndirectOffsetOnAxis(ap=g_put, axis=0),
                            in_=g_new[:, 0:widths[n]], in_offset=None,
                            bounds_check=NP - 1, oob_is_err=False).then_inc(s["g_put"], 16)
                        wait_apart(pool, (s["g_put"], (k + 1) * 16))
                        pool.sem_inc(s["g_free"], 1)
                    pool.sem_inc(pass_done[n], 1)
                s = nodes[n + 1]
                for part, (lo, hi) in enumerate(PARTS):
                    pool.wait_ge(sums_back[part], 16 * (n + 1))
                    with pool.Fori(lo, hi) as i:
                        if n == 0:
                            cnt = A[:, ds(i * TB, TB), C_ONE:C_ONE + 1].broadcast_to([P, TB, F])
                            pool.tensor_tensor(blk(Q, i), blk(Q, i), cnt, ALU.mult).then_inc(s["half"], 1)
                            pool.wait_ge(s["half"], i + 1)
                            pool.tensor_tensor(blk(X, i), blk(X, i), blk(Q, i), ALU.add).then_inc(s["added"], 1)
                        else:
                            sums_blk = A[:, ds(i * TB, TB), 0:F]
                            pool.tensor_tensor(sums_blk, sums_blk, blk(G, i), ALU.add).then_inc(s["added"], 1)
            s = nodes[3]
            with pool.Fori(0, NB) as i:
                pool.wait_ge(s["normed"], 2 * i + 3)
                pool.tensor_tensor(blk(H, i), blk(H, i), blk(X, i), ALU.add).then_inc(s["made"], 1)

        @block.scalar
        def _(act):
            act.dma_start(ident[:, :], c["identity"]).then_inc(ident_ready, 16)
            act.dma_start(W14[:, 0:F], c["L0_gnn_W1"]).then_inc(ld_const, 16)
            act.dma_start(W14[:, F:2 * F], c["L0_gnn_W4"]).then_inc(ld_const, 16)
            act.dma_start(WG[0][:, :], c["L1_gnn_W1"]).then_inc(ld_const, 16)
            act.dma_start(WG[1][:, :], c["L1_gnn_W2"]).then_inc(ld_const, 16)
            act.dma_start(vec["w2"][:, :], c["L0_gnn_W2"].rearrange("f a -> (f a)").partition_broadcast(P)).then_inc(ld_const, 16)
            act.dma_start(b2col[:, :], c["L0_gnn_b2"].partition_broadcast(P)).then_inc(ld_const, 16)
            for v, name in (("b1", "L0_gnn_b1"), ("b4", "L0_gnn_b4"), ("c1", "L1_gnn_b1"), ("gm1", "L1_gnn_gamma1"),
                            ("bt1", "L1_gnn_beta1"), ("c2", "L1_gnn_b2"), ("gm2", "L1_gnn_gamma2"), ("bt2", "L1_gnn_beta2")):
                act.dma_start(vec[v][:, :], c[name].partition_broadcast(P)).then_inc(ld_const, 16)
            act.wait_ge(ld_const, 16 * 14)

            def transform(s, from_x):
                act.sem_inc(s["hT_ready"], 1)
                with act.Fori(0, NB) as i:
                    act.wait_ge(s["tr_done"], i + 1)
                    if from_x:
                        if s is nodes[0]:
                            act.wait_ge(s["h_copied"], i + 1)
                        for t in range(TB):
                            at = ds(i * TB + t, 1)
                            done = act.activation(stage[:, t, :], tile_of(X, i, t), ACT.Relu, bias=nmr[:, at], scale=rstd[:, at])
                        done.then_inc(s["stage_ready"], 1)
                    else:
                        act.wait_ge(s["normed"], 2 * i + 3)
                        act.activation(stage[:, :, :], tmpb, ACT.Relu).then_inc(s["stage_ready"], 1)
                    act.wait_ge(s["tr_done"], i + 2)
                    act.wait_ge(s["mm_done"], i + 1)
                    act.activation(hT[:, :, :], psT[:, :, :], ACT.Copy).then_inc(s["hT_ready"], 1)

            def std(s):
                phase = nodes.index(s) + 1
                act.wait_ge(stat, phase)
                act.activation(rstd[:, :], rstd[:, :], ACT.Sqrt).then_inc(sd, 1)
                act.wait_ge(rs, phase)

            std(nodes[0])
            transform(nodes[0], True)

            windowed = is_windowed(act)
            for n in range(3):
                s = passes[n]
                w = widths[n]
                with act.If(windowed):
                    act.wait_ge(tables_ready[n], 1)
                    for b in range(2):
                        act.sem_inc(s["stored"][b], 16)
                    if n == 0:
                        for u in range(2 * U):
                            act.sem_inc(s["rows_used"][u], 1)
                        act.sem_inc(s["sig"], 2)

                    def gate_rows(i, b, h):
                        u = U * b + h
                        if h == 0:
                            act.wait_ge(s["acc_done"][b], i + 1)
                            act.wait_ge(s["oh_ready"][b], i + 2)
                        act.wait_ge(s["z_ready"][h], 2 * i + (b + 1))
                        act.activation(V[b][:, h * KU:(h + 1) * KU, C_W:C_W + 1], z[h][:, :].unsqueeze(2),
                                       ACT.Sigmoid, bias=b2col[:, 0:1]).then_inc(s["sig"], 1)
                        act.wait_ge(s["sig"], 4 * i + (2 * b + h + 3))
                        for j in range(KU):
                            jj = h * KU + j
                            done = act.activation(V[b][:, jj, 0:F], rows[u][:, j, F:2 * F], ACT.Copy,
                                                  scale=V[b][:, jj, C_W:C_W + 1])
                        done.then_inc(s["rows_used"][u], 1)

                    def store_window(i, b):
                        g = 2 * i + b
                        first = first_node(act, g)
                        act.wait_ge(s["acc_done"][b], i + 2)
                        act.wait_ge(s["stored"][b], (i + 1) * 16)
                        act.activation(R[b][:, 0:w], psA[b][:, 0:w], ACT.Copy).then_inc(s["R_ready"][b], 1)
                        act.wait_ge(s["R_ready"][b], i + 2)
                        act.wait_ge(s["stored"][1 - b], (i + (1 + b)) * 16)
                        act.dma_start(sums[n][ds(first, P), :], R[b][:, 0:w]).then_inc(s["stored"][b], 16)

                    if n == 0:
                        act.preload_act_table(ACT.Sigmoid)
                        gate_rows(0, 0, 0)
                        gate_rows(0, 0, 1)
                        with act.Fori(0, NIT - 1) as i:
                            gate_rows(i, 1, 0)
                            store_window(i, 0)
                            gate_rows(i, 1, 1)
                            gate_rows(i + 1, 0, 0)
                            store_window(i, 1)
                            gate_rows(i + 1, 0, 1)
                        gate_rows(NIT - 1, 1, 0)
                        store_window(NIT - 1, 0)
                        gate_rows(NIT - 1, 1, 1)
                        store_window(NIT - 1, 1)
                    else:
                        with act.Fori(0, NIT) as i:
                            for b in range(2):
                                store_window(i, b)
                    for b in range(2):
                        act.wait_ge(s["stored"][b], 16 * (NIT + 1))
                    act.sem_inc(pass_done[n], 1)
                with act.Else():
                    if n == 0:
                        with act.Fori(0, NCH) as k:
                            act.wait_ge(s["g_z"], k + 1)
                            act.activation(g_v[:, C_W:C_W + 1], g_z, ACT.Sigmoid, bias=b2col[:, 0:1]).then_inc(s["g_w"], 1)
                s = nodes[n + 1]
                if n == 0:
                    act.wait_ge(s["add"], 1)
                    act.activation(dinv[:, :], dinv[:, :], ACT.Sqrt).then_inc(scaled, 1)
                std(s)
                if n < 2:
                    transform(s, n == 0)

        @block.tensor
        def _(pe):
            pe.wait_ge(ident_ready, 16)
            pe.wait_ge(pro, 8)
            pe.transpose(psT[0:1, 0, :], bad[:, :], ident[:, :]).then_inc(bad_T, 1)
            pe.wait_ge(delta_ready, 1)
            pe.matmul(psA[0][:, 0:NGP], ones_row[:, :], delta_row[:, :], start=True, stop=True).then_inc(delta_mm, 1)
            pe.wait_ge(ld_const, 16 * 14)
            pe.wait_ge(flag_ready, 1)

            def transform(s, weight, width):
                pe.sem_inc(s["tr_done"], 1)
                pe.sem_inc(s["mm_done"], 1)
                with pe.Fori(0, NB) as i:
                    pe.wait_ge(s["stage_ready"], i + 1)
                    pe.wait_ge(s["hT_ready"], i + 1)
                    for t in range(TB):
                        done = pe.transpose(psT[:, t, :], stage[:, t, :], ident[:, :])
                    done.then_inc(s["tr_done"], 1)
                    pe.wait_ge(s["hT_ready"], i + 2)
                    pe.wait_ge(s["out_done"], i + 1)
                    for t in range(TB):
                        done = pe.matmul(psO[:, t, 0:width], hT[:, t, :], weight[:, :], start=True, stop=True)
                    done.then_inc(s["mm_done"], 1)

            transform(nodes[0], W14, 2 * F)

            windowed = is_windowed(pe)
            for n in range(3):
                s = passes[n]
                w = widths[n]
                with pe.If(windowed):
                    for b in range(2):
                        pe.sem_inc(s["acc_done"][b], 1)
                    if n:
                        for u in range(2 * U):
                            pe.sem_inc(s["rows_used"][u], 1)

                    def at_dst(i, b, h, back):
                        i = i + back
                        pe.wait_ge(s["ohT_ready"][b], i + 1)
                        pe.wait_ge(s["pwin_ready"][b], (i + 1) * 16)
                        pe.wait_ge(s["psE_free"][h], 2 * i + (b + 1))
                        for j in range(KU):
                            for part in range(3):
                                done = pe.matmul(psE[h][:, j, :], ohT[b][:, h * KU + j, :],
                                                 pwin[b][:, part * F:(part + 1) * F],
                                                 start=(part == 0), stop=(part == 2))
                        done.then_inc(s["psE_ready"][h], 1)

                    def sum_unit(i, b, h):
                        u = U * b + h
                        if n == 0:
                            pe.wait_ge(s["rows_used"][u], i + 2)
                        else:
                            pe.wait_ge(s["rows_ready"][u], (i + 1) * 16 * KU)
                        for j in range(KU):
                            jj = h * KU + j
                            value = V[b][:, jj, 0:w] if n == 0 else rows[u][:, j, 0:F]
                            done = pe.matmul(psA[b][:, 0:w], oh[b][:, jj, :], value, start=(jj == 0), stop=False)
                        if n:
                            done.then_inc(s["rows_used"][u], 1)

                    if n == 0:
                        for h in range(U):
                            at_dst(0, 0, h, 0)
                    with pe.Fori(0, NIT) as i:
                        for b in range(2):
                            for h in range(U):
                                if n == 0:
                                    at_dst(i, 1 - b, h, b)
                                if h == 0:
                                    pe.wait_ge(s["oh_ready"][b], i + 2)
                                    pe.wait_ge(s["R_ready"][b], i + 1)
                                sum_unit(i, b, h)
                            pe.wait_ge(s["R_ready"][1 - b], i + 1 + b)
                            pe.matmul(psA[b][:, 0:w], shift[b][:, :], R[1 - b][:, 0:w], start=False, stop=True)\
                              .then_inc(s["acc_done"][b], 1)
                with pe.Else():
                    with pe.Fori(0, NCH) as k:
                        pe.wait_ge(s["g_v"], k + 1)
                        pe.matmul(psA[0][:, 0:w], g_eq, g_v[:, 0:w], start=True, stop=True).then_inc(s["g_mm"], 1)
                if n < 2:
                    transform(nodes[n + 1], WG[n], F)

        @block.vector
        def _(dve):
            dve.memset(zeros, 0.0).then_inc(zeros_ready, 1)
            dve.memset(ones_row[:, :], 1.0)
            dve.memset(bad[:, :], -1.0)
            for b in range(2):
                dve.memset(V[b][:, :, C_ONE:C_ONE + 1], 1.0)
            dve.wait_ge(iotas, 3)
            dve.tensor_scalar(below[:, :], iota_dif[:, :], 0.0, None, ALU.is_gt)

            dve.wait_ge(ld_edge, 32)
            dve.tensor_copy(basef[:, :].unsqueeze(2), by_group(dst_i)[:, :, 0:1]).then_inc(pro, 1)
            dve.tensor_tensor(gap, nxt_i, dst_i, ALU.subtract).then_inc(pro, 1)
            dve.wait_ge(pro, 1)
            dve.sem_inc(base_ready, 1)
            dve.tensor_tensor(span[:, :].unsqueeze(2), by_group(dst_i)[:, :, GE - 1:GE], basef[:, :].unsqueeze(2),
                              ALU.subtract).then_inc(pro, 1)
            dve.wait_ge(pro, 3)
            dve.tensor_reduce(small[:, 0:1], gap, AX.X, ALU.min).then_inc(pro, 1)
            dve.tensor_reduce(small[:, 1:2], span[:, :], AX.X, ALU.max).then_inc(pro, 1)
            dve.wait_ge(pro, 5)
            dve.tensor_scalar(small[:, 2:3], small[:, 1:2], float(1 - P), None, ALU.add).then_inc(pro, 1)
            dve.tensor_scalar(small[:, 3:4], small[:, 0:1], -1.0, None, ALU.mult).then_inc(pro, 1)
            dve.wait_ge(pro, 7)
            dve.tensor_tensor(bad[0:GROWS, :], small[:, 2:3], small[:, 3:4], ALU.max).then_inc(pro, 1)
            dve.wait_ge(bad_T, 1)
            dve.tensor_reduce(badmax[:, :], psT[0:1, 0, :], AX.X, ALU.max).then_inc(pro, 1)
            dve.wait_ge(pro, 9)
            dve.tensor_scalar(flag[:, :], badmax[:, :], 0.0, None, ALU.is_le).then_inc(flag_ready, 1)
            dve.memset(delta_row[:, 0:1], 0.0)
            dve.wait_ge(base_back, 32)
            dve.tensor_copy(first_i[:, :], base_row[:, :])
            dve.tensor_tensor(delta_row[:, 1:NGP], base_row[:, 1:NGP], base_row[:, 0:NGP - 1], ALU.subtract)\
               .then_inc(delta_ready, 1)
            dve.wait_ge(delta_mm, 1)
            dve.tensor_copy(delta[:, :], psA[0][:, 0:NGP]).then_inc(pro, 1)
            dve.wait_ge(pro, 10)
            dve.wait_ge(ld_const, 16 * 14)

            def block_stats(s, i, t):
                for q in range(TB):
                    done = dve.bn_stats(stats[:, q, :], tile_of(t, i, q))
                done.then_inc(s["own2"], 1)
                wait_apart(dve, (s["own2"], 3 * i + 1))
                for q in range(TB):
                    done = dve.bn_aggr(mvb[:, q, :], stats[:, q, :])
                done.then_inc(s["own2"], 1)
                dve.wait_ge(s["own2"], 3 * i + 2)
                dve.tensor_copy(blk(mv, i), mvb[:, :, :]).then_inc(s["own2"], 1)

            def finish_stats(s):
                phase = nodes.index(s) + 1
                dve.wait_ge(s["own2"], 3 * NB)
                dve.tensor_scalar(rstd[:, :].unsqueeze(2), mv[:, :, 1:2], EPS, None, ALU.add).then_inc(stat, 1)
                dve.wait_ge(sd, phase)
                dve.reciprocal(rstd[:, :], rstd[:, :]).then_inc(norm, 1)
                dve.wait_ge(norm, phase)
                dve.scalar_tensor_tensor(nmr[:, :].unsqueeze(2), mv[:, :, 0:1], -1.0, rstd[:, :].unsqueeze(2),
                                         ALU.mult, ALU.mult).then_inc(rs, 1)
                dve.wait_ge(rs, phase)

            s = nodes[0]
            dve.wait_ge(ld_x, 16)
            with dve.Fori(0, NB) as i:
                block_stats(s, i, X)
            finish_stats(s)
            dve.sem_inc(s["out_done"], 1)
            dve.sem_inc(s["row_stored"], 16)
            dve.sem_inc(s["win_stored"], 16)
            with dve.Fori(0, NB) as i:
                dve.wait_ge(s["mm_done"], i + 2)
                dve.wait_ge(s["row_stored"], 16 * i + 16)
                dve.tensor_tensor(tst[:, :, 0:F], psO[:, :, 0:F], per_feature(vec["b1"]), ALU.subtract).then_inc(s["p_made"], 1)
                dve.wait_ge(s["win_stored"], 16 * i + 16)
                dve.tensor_copy(pw3[:, :, 0:F], psO[:, :, 0:F]).then_inc(s["own"], 1)
                dve.wait_ge(s["own"], 3 * i + 1)
                dve.tensor_tensor(pres[:, :, :], psO[:, :, 0:F], pw3[:, :, 0:F], ALU.subtract).then_inc(s["own"], 1)
                dve.tensor_tensor(blk(Q, i), psO[:, :, F:2 * F], per_feature(vec["b4"]), ALU.add).then_inc(s["out_done"], 1)
                dve.wait_ge(s["own"], 3 * i + 2)
                dve.tensor_copy(pw3[:, :, F:2 * F], pres[:, :, :]).then_inc(s["own"], 1)
                dve.wait_ge(s["own"], 3 * i + 3)
                dve.tensor_tensor(pw3[:, :, 2 * F:3 * F], pres[:, :, :], pw3[:, :, F:2 * F], ALU.subtract)\
                   .then_inc(s["pw_made"], 1)

            windowed = is_windowed(dve)
            for n in range(3):
                s = passes[n]
                w = widths[n]
                with dve.If(windowed):
                    dve.memset(R[1][:, :], 0.0).then_inc(s["R_ready"][1], 1)
                    dve.sem_inc(s["R_ready"][0], 1)
                    for b in range(2):
                        dve.sem_inc(s["oh_ready"][b], 1)
                        if n == 0:
                            dve.sem_inc(s["psE_free"][b], 1)

                    def one_hot_rows(i, b, back):
                        i = i + back
                        dve.wait_ge(s["rel_ready"][b], (i + 1) * 48)
                        dve.tensor_scalar(ohT[b][:, :, :], relr[b][:, :].rearrange("p (j e) -> p j e", j=K),
                                          iota_col[:, 0:1], None, ALU.is_equal).then_inc(s["ohT_ready"][b], 1)

                    def one_hots(i, b, back):
                        i = i + back
                        g = 2 * i + b
                        if n:
                            dve.wait_ge(s["rel_ready"][b], (i + 1) * 32)
                        dve.wait_ge(s["acc_done"][b], i + 1)
                        node = iota_row[:, :].unsqueeze(1).broadcast_to([P, K, P])
                        rel = relp[b][:, :].unsqueeze(2).broadcast_to([P, K, P])
                        dve.tensor_scalar(shift[b][:, :], iota_dif[:, :], delta[:, ds(g, 1)], None, ALU.is_equal)
                        if n == 0:
                            dve.tensor_copy(V[b][:, :, C_EW:C_EW + 1], eww[b][:, :].unsqueeze(2))
                            dve.tensor_tensor(oh[b][:, :, :], node, rel, ALU.is_equal).then_inc(s["oh_ready"][b], 1)
                        else:
                            dve.wait_ge(s["oh_ready"][1 - b], i + (1 + b))
                            dve.tensor_tensor(eqm[:, :, :], node, rel, ALU.is_equal).then_inc(s["eq"][b], 1)
                            dve.wait_ge(s["eq"][b], i + 1)
                            dve.tensor_tensor(oh[b][:, :, :], eqm[:, :, :], eww[b][:, :].unsqueeze(2).broadcast_to([P, K, P]),
                                              ALU.mult).then_inc(s["oh_ready"][b], 1)

                    def gate_sums(i, b, h):
                        u = U * b + h
                        dve.wait_ge(s["psE_ready"][h], 2 * i + (b + 1))
                        dve.wait_ge(s["rows_ready"][u], (i + 1) * 16 * KU)
                        dve.tensor_tensor(diff[:, :, :], psE[h][:, :, :], rows[u][:, :, 0:F], ALU.subtract)\
                           .then_inc(s["psE_free"][h], 1)
                        dve.wait_ge(s["psE_free"][h], 2 * i + (b + 2))
                        dve.scalar_tensor_tensor(gated[:, :, :], diff[:, :, :], 0.0, per_feature(vec["w2"]),
                                                 ALU.max, ALU.mult).then_inc(s["gated"], 1)
                        dve.wait_ge(s["gated"], 4 * i + (2 * b + h + 1))
                        dve.wait_ge(s["sig"], 4 * i + (2 * b + h + 1))
                        dve.tensor_reduce(z[h][:, :], gated[:, :, :], AX.X, ALU.add).then_inc(s["z_ready"][h], 1)

                    if n == 0:
                        one_hot_rows(0, 0, 0)
                        one_hots(0, 0, 0)
                        with dve.Fori(0, NIT) as i:
                            for b in range(2):
                                one_hot_rows(i, 1 - b, b)
                                gate_sums(i, b, 0)
                                one_hots(i, 1 - b, b)
                                gate_sums(i, b, 1)
                    else:
                        with dve.Fori(0, NIT) as i:
                            for b in range(2):
                                one_hots(i, b, 0)
                with dve.Else():
                    OWN = 8 if n == 0 else 4
                    gathers = 2 if n == 0 else 1
                    dve.sem_inc(s["g_free"], 1)
                    with dve.Fori(0, NCH) as k:
                        own = lambda m: dve.wait_ge(s["g_own"], k * OWN + m)
                        dve.wait_ge(s["g_nodes"], (k + 1) * 32)
                        dve.wait_ge(s["g_edges"], (k + 1) * 32)
                        dve.tensor_copy(g_dstf, g_dst).then_inc(s["g_own"], 1)
                        own(1)
                        dve.tensor_scalar(g_eq, g_row, g_dstf, None, ALU.is_equal).then_inc(s["g_own"], 1)
                        own(2)
                        dve.tensor_tensor(g_low, g_eq, below[:, :], ALU.mult).then_inc(s["g_own"], 1)
                        own(3)
                        dve.tensor_reduce(g_cnt, g_low, AX.X, ALU.max).then_inc(s["g_own"], 1)
                        own(4)
                        dve.scalar_tensor_tensor(g_put, g_cnt, float(2 * NP), g_dstf, ALU.mult, ALU.add)
                        dve.wait_ge(s["g_rows"], (k + 1) * (16 * gathers))
                        if n == 0:
                            dve.tensor_tensor(diff[:, 0, :], g_to[:, 0:F], g_from[:, 0:F], ALU.subtract).then_inc(s["g_own"], 1)
                            own(5)
                            dve.tensor_tensor(diff[:, 1, :], diff[:, 0, :], vec["b1"][:, :], ALU.add).then_inc(s["g_own"], 1)
                            own(6)
                            dve.scalar_tensor_tensor(gated[:, 0, :], diff[:, 1, :], 0.0, vec["w2"][:, :], ALU.max, ALU.mult)\
                               .then_inc(s["g_own"], 1)
                            own(7)
                            dve.tensor_reduce(g_z, gated[:, 0, :], AX.X, ALU.add).then_inc(s["g_z"], 1)
                            dve.tensor_copy(g_v[:, C_EW:C_EW + 1], g_ew).then_inc(s["g_own"], 1)
                            dve.wait_ge(s["g_w"], k + 1)
                            own(8)
                            dve.tensor_scalar(g_v[:, 0:F], g_from[:, F:2 * F], g_v[:, C_W:C_W + 1], None, ALU.mult)\
                               .then_inc(s["g_v"], 1)
                        else:
                            dve.tensor_scalar(g_v[:, 0:F], g_from[:, 0:F], g_ew, None, ALU.mult).then_inc(s["g_v"], 1)
                        dve.wait_ge(s["g_mm"], k + 1)
                        dve.wait_ge(s["g_sums"], (k + 1) * 16)
                        dve.tensor_tensor(g_new[:, 0:w], psA[0][:, 0:w], g_acc[:, 0:w], ALU.add).then_inc(s["g_new"], 1)

                s = nodes[n + 1]
                bias, gamma, beta = (vec[v + str(n)] if n else None for v in ("c", "gm", "bt"))
                rows_in = H if n else X
                for part, (lo, hi) in enumerate(PARTS):
                    dve.wait_ge(sums_back[part], 16 * (n + 1))
                    if n == 0 and part == 0:
                        dve.wait_ge(ld_h, 16)
                    with dve.Fori(lo, hi) as i:
                        if n == 0:
                            for q in range(TB):
                                t = ds(i * TB + q, 1)
                                sw = A[:, t, C_W:C_W + 1].rearrange("p a f -> p (a f)")
                                done = dve.scalar_tensor_tensor(tile_of(H, i, q), tile_of(H, i, q), sw, tile_of(A, i, q),
                                                                ALU.mult, ALU.subtract)
                            done.then_inc(s["own"], 1)
                            dve.wait_ge(s["own"], 2 * i + 1)
                            dve.wait_ge(s["added"], i + 1)
                            dve.tensor_tensor(blk(X, i), blk(X, i), blk(H, i), ALU.add).then_inc(s["own"], 1)
                            wait_apart(dve, (s["own"], 2 * i + 2))
                        else:
                            dve.wait_ge(s["added"], i + 1)
                            for q in range(TB):
                                done = dve.scalar_tensor_tensor(tile_of(H, i, q), tile_of(A, i, q), dinv[:, ds(i * TB + q, 1)],
                                                                bias[:, :], ALU.mult, ALU.add)
                            done.then_inc(s["own"], 1)
                            wait_apart(dve, (s["own"], i + 1))
                        block_stats(s, i, rows_in)
                if n == 0:
                    dve.tensor_scalar(dinv[:, :].unsqueeze(2), A[:, :, C_EW:C_EW + 1], 1.0, None, ALU.add).then_inc(s["add"], 1)
                    dve.wait_ge(scaled, 1)
                    dve.reciprocal(dinv[:, :], dinv[:, :]).then_inc(s["own"], 1)
                    dve.wait_ge(s["own"], 2 * NB + 1)
                finish_stats(s)

                def normed(i, into):
                    dve.wait_ge(s["normed"], 2 * i + 1)
                    for q in range(TB):
                        mean = mv[:, ds(i * TB + q, 1), 0:1].rearrange("p a f -> p (a f)")
                        done = dve.scalar_tensor_tensor(tmpa[:, q, :], tile_of(H, i, q), mean, gamma[:, :],
                                                        ALU.subtract, ALU.mult)
                    done.then_inc(s["normed"], 1)
                    dve.wait_ge(s["normed"], 2 * i + 2)
                    for q in range(TB):
                        done = dve.scalar_tensor_tensor(into(q), tmpa[:, q, :], rstd[:, ds(i * TB + q, 1)], beta[:, :],
                                                        ALU.mult, ALU.add)
                    done.then_inc(s["normed"], 1)

                def scale_out(i):
                    dve.wait_ge(s["mm_done"], i + 2)
                    dve.tensor_tensor(blk(G, i), psO[:, :, 0:F], per_node(dinv, i), ALU.mult).then_inc(s["out_done"], 1)

                if n < 2:
                    dve.sem_inc(s["out_done"], 1)
                if n > 0:
                    dve.sem_inc(s["normed"], 1)
                if n == 0:
                    with dve.Fori(0, NB) as i:
                        scale_out(i)
                elif n == 1:
                    to_relu = lambda q: tmpb[:, q, :]
                    normed(0, to_relu)
                    with dve.Fori(1, NB) as i:
                        dve.wait_ge(s["stage_ready"], i)
                        normed(i, to_relu)
                        scale_out(i - 1)
                    scale_out(NB - 1)
                else:
                    with dve.Fori(0, NB) as i:
                        normed(i, lambda q: tile_of(H, i, q))


_WEIGHTS = ["L0_gnn_W1", "L0_gnn_b1", "L0_gnn_W2", "L0_gnn_b2", "L0_gnn_W4", "L0_gnn_b4", "L1_gnn_W1", "L1_gnn_b1",
            "L1_gnn_gamma1", "L1_gnn_beta1", "L1_gnn_W2", "L1_gnn_b2", "L1_gnn_gamma2", "L1_gnn_beta2"]


def kernel(**inputs):
    import numpy as np
    import concourse.bacc as bacc
    from concourse.bass_utils import run_bass_kernel_spmd

    def padded(a, n, value):
        out = np.full((n,) + a.shape[1:], value, a.dtype)
        out[:a.shape[0]] = a
        return out

    arrays = {
        "x": padded(np.asarray(inputs["x"]), NP, 0),
        "src": padded(np.asarray(inputs["src"]), EP, 0),
        "dst": padded(np.asarray(inputs["dst"]), EP + 1, N),
        "edge_weight": padded(np.asarray(inputs["edge_weight"]), EP, 0),
        "identity": np.eye(P, dtype=np.float32),
    }
    for name in _WEIGHTS:
        arrays[name] = np.ascontiguousarray(inputs[name])

    nc = bacc.Bacc("TRN2", target_bir_lowering=False, num_devices=1)
    args = {}
    for name, a in arrays.items():
        args[name] = nc.dram_tensor(f"in_{name}", a.shape, mybir.dt.from_np(a.dtype), kind="ExternalInput").ap()
    out = nc.dram_tensor("out_x", (N, F), F32, kind="ExternalOutput").ap()
    build_program(nc, args["x"], args["src"], args["dst"], args["edge_weight"], args, out)
    r = run_bass_kernel_spmd(nc, [{f"in_{k}": v for k, v in arrays.items()}], core_ids=[0])
    return r.results[0]["out_x"]
```

```python
from contextlib import ExitStack
from functools import partial

import concourse.bass as bass
from concourse import mybir

F32, BF16, I32 = mybir.dt.float32, mybir.dt.bfloat16, mybir.dt.int32
ALU = mybir.AluOpType
ACT = mybir.ActivationFunctionType
AX = mybir.AxisListType

N = 6250
F = 128
E = 206250
P = 128
EPS = 1e-5

K = 8
GE = K * P
NG = -(-E // GE)
NG += NG % 2
assert NG % 4 == 2
NIT = NG // 2
NGP = NG + 2
EP = NGP * GE
GPP = 2
GROWS = NGP // GPP
U = 2
KU = K // U

TB = 4
NB = -(-(N + P) // (TB * P))
NT = NB * TB
NP = NT * P

NODE_TILES = -(-N // P)
QUADS = NG // 4
LAG = 4
XPARTS = (0, 4, 9, NB)
EARLY = QUADS - LAG
LATE = NODE_TILES - EARLY - 1
LAST = NODE_TILES - 1
OWN_STEPS = (6, 6, 7)

C_W, C_ONE, C_EW = F, F + 1, F + 2
AW = F + 3
NCH = NG * K


def ds(start, size):
    return bass.ds(start, size)


def build_program(nc, x, src, dst, ew, c, out):
    table0 = nc.dram_tensor("table0", (NP, 2 * F), F32).ap()
    pwin_d = nc.dram_tensor("pwin_d", (NP, 3 * F), BF16).ap()
    table1 = nc.dram_tensor("table1", (NODE_TILES * P, F), F32).ap()
    table2 = nc.dram_tensor("table2", (NODE_TILES * P, F), F32).ap()
    sums0 = nc.dram_tensor("sums0", (NP, AW), F32).ap()
    sums1 = nc.dram_tensor("sums1", (NP, F), F32).ap()
    sums2 = nc.dram_tensor("sums2", (NP, F), F32).ap()
    relp_d = nc.dram_tensor("relp_d", (EP,), F32).ap()
    relr_d = nc.dram_tensor("relr_d", (EP,), BF16).ap()
    base_d = nc.dram_tensor("base_d", (NGP,), F32).ap()
    fits_d = nc.dram_tensor("fits_d", (GROWS,), F32).ap()

    ctx = ExitStack()
    with ctx:
        def sb(name, shape, dt=F32):
            return ctx.enter_context(nc.sbuf_tensor(name, shape, dt))

        def pb(name, shape, dt=F32):
            return ctx.enter_context(nc.psum_tensor(name, shape, dt))

        def sem(name):
            return ctx.enter_context(nc.semaphore(name))

        X = sb("X", [P, NT, F])
        A = sb("A", [P, NT, AW])
        H = sb("H", [P, NT, F])
        Q = sb("Q", [P, NT, F])
        G = sb("G", [P, NT, F])
        mv = sb("mv", [P, NT, 2])
        rstd = sb("rstd", [P, NT])
        nmr = sb("nmr", [P, NT])
        dinv = sb("dinv", [P, NT])
        g_i32 = G[:, :, :].rearrange("p t f -> p (t f)").bitcast(I32)
        SP_E = GPP * GE
        dst_i = g_i32[0:GROWS, 0:SP_E]
        nxt_i = g_i32[0:GROWS, SP_E:2 * SP_E]
        gap = G[:, :, :].rearrange("p t f -> p (t f)")[0:GROWS, 2 * SP_E:3 * SP_E]
        a_f32 = A[:, :, :].rearrange("p t f -> p (t f)")
        relp_all = a_f32[0:GROWS, 0:SP_E]
        relr_all = a_f32[0:GROWS, SP_E:SP_E + SP_E // 2].bitcast(BF16)
        stats_x = a_f32[:, SP_E + SP_E // 2:SP_E + SP_E // 2 + NT * 6].rearrange("p (t c) -> p t c", c=6)

        ident = sb("ident", [P, P])
        iota_row = sb("iota_row", [P, P])
        iota_col = sb("iota_col", [P, 1])
        iota_dif = sb("iota_dif", [P, P])
        below = sb("below", [P, P])
        W14 = sb("W14", [P, 2 * F])
        WG = [sb("WG1", [P, F]), sb("WG2", [P, F])]
        vec = {n: sb("v_" + n, [P, F]) for n in ("b1", "w2", "b4", "c1", "gm1", "bt1", "c2", "gm2", "bt2")}
        b2col = sb("b2col", [P, 1])
        basef = sb("basef", [GROWS, GPP])
        span = sb("span", [GROWS, GPP])
        small = sb("small", [GROWS, 4])
        fits = sb("fits", [GROWS, 1])
        flag = sb("flag", [1, 1], I32)
        first_i = sb("first_i", [1, NGP], I32)
        worst = sb("worst", [1, 1])
        delta = sb("delta", [P, NGP])
        stats = sb("stats", [P, TB, 6])
        mvb = sb("mvb", [P, TB, 2])
        var = sb("var", [P, TB, 2])
        sdev = sb("sdev", [P, TB, 2])
        inv = sb("inv", [P, TB, 2])
        nmrb = sb("nmrb", [P, TB])
        stage = sb("stage", [P, TB, F])
        hT = sb("hT", [P, TB, P])
        tst = [sb(f"tst{b}", [P, TB, F]) for b in range(2)]
        idx = [sb(f"idx{b}", [P, K], I32) for b in range(2)]
        relp = [sb(f"relp{b}", [P, K]) for b in range(2)]
        relr = [sb(f"relr{b}", [P, GE], BF16) for b in range(2)]
        eww = [sb(f"eww{b}", [P, K]) for b in range(2)]
        pwin = [sb(f"pwin{b}", [P, 3 * F], BF16) for b in range(2)]
        rows = [sb(f"rows{u}", [P, KU, 2 * F]) for u in range(2 * U)]
        ohT = [sb(f"ohT{b}", [P, K, P], BF16) for b in range(2)]
        oh = [sb(f"oh{b}", [P, K, P]) for b in range(2)]
        eqm = sb("eqm", [P, K, P])
        shift = [sb(f"shift{b}", [P, P]) for b in range(2)]
        diff = sb("diff", [P, KU, F])
        gated = sb("gated", [P, KU, F])
        z = [sb(f"z{h}", [P, KU]) for h in range(U)]
        V = [sb(f"V{b}", [P, K, AW]) for b in range(2)]
        R = [sb(f"R{b}", [P, AW]) for b in range(2)]
        pres = [diff, gated]
        pw3 = [oh[b][:, :, :].rearrange("p a b -> p (a b)").bitcast(BF16)[:, 0:TB * 3 * F]
               .rearrange("p (t c) -> p t c", t=TB) for b in range(2)]
        stage_a = [stage, eqm[:, 0:TB, :]]
        hT_a = [hT, eqm[:, TB:2 * TB, :]]
        eq_f32 = a_f32[:, SP_E + SP_E // 2 + NT * 6:]
        base_all = eq_f32[:, 0:NGP]
        need = eq_f32[0:1, NGP:NGP + EARLY]
        slack = eq_f32[0:1, NGP + EARLY:NGP + EARLY + GROWS + EARLY + (NG - 1) + 2]

        g_dst = idx[1][:, 0:1]
        g_src = idx[0][:, 0:1]
        g_put = idx[1][:, 1:2]
        g_ew = eww[0][:, 0:1]
        g_dstf = eww[0][:, 1:2]
        g_cnt = eww[0][:, 2:3]
        g_z = eww[0][:, 4:5]
        g_row = eqm[:, 0, :].bitcast(I32)
        g_eq = oh[0][:, 0, :]
        g_low = oh[0][:, 1, :]
        g_from = rows[0][:, 0, :]
        g_to = rows[1][:, 0, :]
        g_acc = R[0]
        g_new = R[1]
        g_v = V[0][:, 0, :]
        zeros = oh[1][:, :, :].rearrange("p a b -> p (a b)")[:, 0:TB * AW]

        psE = [pb(f"psE{h}", [P, KU, P]) for h in range(U)]
        psA = [pb(f"psA{b}", [P, 512]) for b in range(2)]
        psT = pb("psT", [P, TB, P])
        psO = pb("psO", [P, TB, 2 * F])

        psT_a = [psT, psE[0]]
        psP_a = [psO[:, 0:TB // 2, :].rearrange("p a (b f) -> p (a b) f", f=F),
                 psA[0][:, :].rearrange("p (t f) -> p t f", f=F)]
        psQ_a = [psO[:, TB // 2:TB, :].rearrange("p a (b f) -> p (a b) f", f=F),
                 psA[1][:, :].rearrange("p (t f) -> p t f", f=F)]

        ld_edge = sem("ld_edge")
        ld_x = [sem(f"ld_x{part}") for part in range(len(XPARTS) - 1)]
        ld_const = sem("ld_const")
        ld_h = sem("ld_h")
        iotas = sem("iotas")
        passed = sem("passed")
        ident_ready = sem("ident_ready")
        pro = sem("pro")
        flag_ready = sem("flag_ready")
        base_ready = sem("base_ready")
        base_stored = sem("base_stored")
        base_back = sem("base_back")
        rel_made = sem("rel_made")
        rel_stored = sem("rel_stored")
        zeros_ready = sem("zeros_ready")
        zeroed = sem("zeroed")
        tables_ready = [sem(f"tables_ready{n}") for n in range(3)]
        pass_done = [sem(f"pass_done{n}") for n in range(3)]
        out_stored = sem("out_stored")

        def node_sems(tag, names):
            return {n: sem(f"{n}_{tag}") for n in names.split()}

        turned = "stage_ready tr_done hT_ready mm_done out_done row_stored "
        nodes = [
            node_sems("a", "own stage_ready tr_done hT_ready p_mm q_mm pw1_made p_made pres_made q_out pool_own pw_made last_pw_made"),
            node_sems("b", "sums_back own var_ready sd_ready normed " + turned),
            node_sems("c", "sums_back own var_ready sd_ready normed " + turned),
            node_sems("d", "sums_back own var_ready sd_ready normed"),
        ]
        stat, sd, norm, rs = sem("stat"), sem("sd"), sem("norm"), sem("rs")
        h_stored = [sem("h_stored0"), sem("h_stored1")]
        p_stored = [sem("p_stored0"), sem("p_stored1")]
        win_stored = [sem("win_stored0"), sem("win_stored1")]

        def pass_sems(n):
            pairs = "idx_ready rel_ready oh_ready acc_done R_ready stored "
            pairs += "pwin_ready ohT_ready psE_ready psE_free z_ready" if n == 0 else "eq"
            s = {name: [sem(f"{name}{n}_{b}") for b in range(2)] for name in pairs.split()}
            s["rows_ready"] = [sem(f"rows_ready{n}_{u}") for u in range(2 * U)]
            s["rows_used"] = [sem(f"rows_used{n}_{u}") for u in range(2 * U)]
            if n == 0:
                s["gated"], s["sig"] = sem("gated0"), sem("sig0")
                s["g_z"], s["g_w"] = s["gated"], s["sig"]
            s["g_nodes"], s["g_edges"] = s["rel_ready"]
            s["g_rows"], s["g_sums"], s["g_put"] = s["rows_ready"][0:3]
            s["g_v"], s["g_new"], s["g_free"] = s["rows_used"][0:3]
            s["g_own"], s["g_mm"] = s["oh_ready"]
            return s

        passes = [pass_sems(n) for n in range(3)]
        tables = [table0, table1, table2]
        sums = [sums0, sums1, sums2]
        widths = [AW, F, F]

        def blk(t, i):
            return t[:, ds(i * TB, TB), :]

        def per_feature(v):
            return v[:, :].unsqueeze(1).broadcast_to([P, TB, F])

        def rows_of(t, i):
            return t[ds(i * (TB * P), TB * P), :].rearrange("(t p) f -> p t f", p=P)

        def by_group(t):
            return t.rearrange("r (g e) -> r g e", g=GPP)

        def tile_of(t, i, q):
            return t[:, ds(i * TB + q, 1), 0:F].rearrange("p a f -> p (a f)")

        def all_rows(t):
            return t.rearrange("(t p) f -> p t f", p=P)

        def wait_apart(e, *waits):
            for semaphore, value in waits:
                e.wait_ge(semaphore, value)
            e.sem_inc(passed, 1)

        def is_windowed(e):
            e.wait_ge(flag_ready, 1)
            return e.value_load(flag[0:1, 0:1], min_val=0, max_val=1) > 0

        def tile_at(t, at, q):
            return t[:, ds(at + q, 1), 0:F].rearrange("p a f -> p (a f)")

        def in_quads(e, pair, tile_steps):
            def quad(q, steps):
                for r in range(2):
                    def step(u):
                        if 4 * r + u in steps:
                            steps[4 * r + u](q - LAG, 1, q - LAG)
                    pair(q * 2 + r, False, step)
            with e.Fori(0, LAG) as q:
                quad(q, {})
            with e.Fori(LAG, QUADS) as q:
                quad(q, tile_steps)
            with e.Fori(NIT - 1, NIT) as i:
                pair(i, True, lambda u: None)

        def first_node(e, g):
            return e.value_load(first_i[:, ds(g, 1)], min_val=0, max_val=N)

        block = ctx.enter_context(nc.Block())

        @block.sync
        def _(sp):
            def load_idx(s, g, b):
                sp.dma_start(idx[b][:, :], src[ds(g * GE, GE)].rearrange("(p j) -> p j", j=K)).then_inc(s["idx_ready"][b], 16)

            two = lambda a: a.rearrange("(g e) -> g e", e=GPP * GE)
            for part in range(len(XPARTS) - 1):
                at = slice(XPARTS[part] * TB, XPARTS[part + 1] * TB)
                sp.dma_start(X[:, at, :], all_rows(x)[:, at, :]).then_inc(ld_x[part], 16)
            sp.dma_start(dst_i, two(dst[0:EP])).then_inc(ld_edge, 16)
            sp.dma_start(nxt_i, two(dst[1:EP + 1])).then_inc(ld_edge, 16)

            for b in range(2):
                load_idx(passes[0], b, b)

            s = nodes[0]

            def store_h(i, b):
                wait_apart(sp, (s["stage_ready"], i + 1))
                sp.dma_start(rows_of(table0, i)[:, :, F:2 * F], stage_a[b][:, :, :]).then_inc(h_stored[b], 16)

            def store_window_parts(i, b):
                wait_apart(sp, (s["pw_made"], i + 3))
                sp.dma_start(rows_of(pwin_d, i), pw3[b]).then_inc(win_stored[b], 16)

            def store_pair(j, blocks=2, ahead=2, first=False):
                for b in range(blocks):
                    i = 2 * j + b
                    if b < ahead:
                        store_h(i + 2, b)
                    if not (first and b == 0):
                        store_window_parts(i - 1, 1 - b)
                    wait_apart(sp, (s["p_made"], i + 1))
                    sp.dma_start(rows_of(table0, i)[:, :, 0:F], tst[b][:, :, :]).then_inc(p_stored[b], 16)

            store_h(0, 0)
            store_h(1, 1)
            store_pair(0, first=True)
            store_pair(1)
            store_pair(2)
            sp.wait_ge(base_ready, 1)
            sp.dma_start(base_d.rearrange("(g e) -> g e", e=GPP), basef[:, :]).then_inc(base_stored, 16)
            sp.dma_start(fits_d.rearrange("(g e) -> g e", e=1), fits[:, :]).then_inc(base_stored, 16)
            sp.wait_ge(base_stored, 32)
            sp.dma_start(base_all, base_d.partition_broadcast(P)).then_inc(base_back, 16)
            sp.dma_start(slack[:, 0:GROWS], fits_d.rearrange("(a g) -> a g", a=1)).then_inc(base_back, 16)
            store_pair(3)
            sp.wait_ge(rel_made, 1)
            sp.dma_start(two(relp_d), relp_all).then_inc(rel_stored, 16)
            sp.dma_start(two(relr_d), relr_all).then_inc(rel_stored, 16)
            store_pair(4)
            store_pair(NB // 2 - 1, ahead=1)
            store_pair(NB // 2, blocks=1, ahead=0)
            for b in range(2):
                sp.wait_ge(h_stored[b], 16 * ((NB + 1 - b) // 2 + 1))
                sp.wait_ge(p_stored[b], 16 * ((NB + 1 - b) // 2 + 1))
            sp.sem_inc(tables_ready[0], 1)
            sp.wait_ge(s["last_pw_made"], 1)
            sp.dma_start(rows_of(pwin_d, NB - 1), pw3[0]).then_inc(win_stored[0], 16)
            for b in range(2):
                sp.wait_ge(win_stored[b], 16 * ((NB + 1 - b) // 2 + 1))
            sp.wait_ge(rel_stored, 32)

            def load_rel(n, s, g, b):
                part = lambda a: a[ds(g * GE, GE)]
                if n == 0:
                    sp.dma_start(relr[b][:, :], part(relr_d).partition_broadcast(P)).then_inc(s["rel_ready"][b], 16)
                sp.dma_start(relp[b][:, :], part(relp_d).rearrange("(p j) -> p j", j=K)).then_inc(s["rel_ready"][b], 16)
                sp.dma_start(eww[b][:, :], part(ew).rearrange("(p j) -> p j", j=K)).then_inc(s["rel_ready"][b], 16)

            def load_pwin(s, first, b):
                sp.dma_start(pwin[b][:, :], pwin_d[ds(first, P), :]).then_inc(s["pwin_ready"][b], 16)

            def load_pair(n, i, before):
                s = passes[n]
                for b in range(2):
                    before(b)
                    g = 2 * i + (b + 2)
                    for u in (U * b, U * b + 1):
                        sp.wait_ge(s["rows_ready"][u], (i + 1) * 16 * KU)
                    load_idx(s, g, b)
                    wait_apart(sp, (s["oh_ready"][b], i + 2))
                    load_rel(n, s, g, b)
                    if n == 0:
                        first = first_node(sp, g)
                        wait_apart(sp, (s["psE_free"][1], 2 * i + (b + 2)))
                        load_pwin(s, first, b)

            def sums_in(n, t, m, k):
                tiles = sums[n][ds(t * P, m * P), :].rearrange("(t p) f -> p t f", p=P)
                sp.dma_start(A[:, ds(t, m), 0:widths[n]], tiles).then_inc(nodes[n + 1]["sums_back"], 16)

            def rows_out(n, t, m, k):
                s = nodes[n + 1]
                if n < 2:
                    wait_apart(sp, (s["out_done"], k + 2))
                    into = tables[n + 1][ds(t * P, m * P), :].rearrange("(t p) f -> p t f", p=P)
                    sp.dma_start(into, G[:, ds(t, m), :]).then_inc(s["row_stored"], 16)
                else:
                    wait_apart(sp, (s["normed"], k + 2))
                    into = out[ds(t * P, m * P), :].rearrange("(t p) f -> p t f", p=P)
                    sp.dma_start(into, H[:, ds(t, m), :]).then_inc(out_stored, 16)

            def last_rows_out(n, t, k):
                if n < 2:
                    rows_out(n, t, NODE_TILES - t, k)
                else:
                    m = NODE_TILES - 1 - t
                    if m:
                        rows_out(n, t, m, k)
                    sp.wait_ge(nodes[3]["normed"], k + 2)
                    sp.dma_start(out[(t + m) * P:N, :], H[0:N - (t + m) * P, t + m, :]).then_inc(out_stored, 16)

            windowed = is_windowed(sp)
            with sp.If(windowed):
                for n in range(3):
                    s = passes[n]
                    for b in range(2):
                        if n:
                            load_idx(s, b, b)
                        load_rel(n, s, b, b)
                        if n == 0:
                            load_pwin(s, first_node(sp, b), b)
                    if n == 0:
                        sp.dma_start(H[:, :, :], all_rows(table0)[:, :, F:2 * F]).then_inc(ld_h, 16)
                    if n:
                        sp.wait_ge(nodes[n]["row_stored"], 16 * (EARLY + 2))
                        sp.sem_inc(tables_ready[n], 1)

                    def quad(q, tile_in, tile_out):
                        def traffic(b):
                            if b == 0 and tile_in:
                                wait_apart(sp, (s["stored"][1], q * 32 - 16))
                                sums_in(n, q - LAG, 1, q - LAG)

                        def traffic2(b):
                            if b == 0 and tile_out:
                                rows_out(n, q - (LAG + 1), 1, q - (LAG + 1))
                        load_pair(n, q * 2, traffic)
                        load_pair(n, q * 2 + 1, traffic2)

                    with sp.Fori(0, LAG) as q:
                        quad(q, False, False)
                    with sp.Fori(LAG, LAG + 1) as q:
                        quad(q, True, False)
                    with sp.Fori(LAG + 1, QUADS) as q:
                        quad(q, True, True)
                    def last_traffic(b):
                        if b == 1:
                            rows_out(n, EARLY - 1, 1, EARLY - 1)
                            sp.wait_ge(s["stored"][1], 16 * NIT)
                            sums_in(n, EARLY, LATE, EARLY)

                    with sp.Fori(NIT - 1, NIT) as i:
                        load_pair(n, i, last_traffic)
                    for b in range(2):
                        sp.wait_ge(s["idx_ready"][b], 16 * (NIT + 1))
                        sp.wait_ge(s["rel_ready"][b], 16 * (3 if n == 0 else 2) * (NIT + 1))
                        if n == 0:
                            sp.wait_ge(s["pwin_ready"][b], 16 * (NIT + 1))
                    for b in range(2):
                        sp.wait_ge(s["stored"][b], 16 * (NIT + 1))
                    sums_in(n, LAST, 1, EARLY + 1)
                    rows_out(n, EARLY, LATE, EARLY)
                    last_rows_out(n, LAST, EARLY + 1)
                sp.wait_ge(out_stored, 16 * (EARLY + 2))
            with sp.Else():
                for b in range(2):
                    sp.wait_ge(passes[0]["idx_ready"][b], 16)
                sp.dma_start(H[:, :, :], all_rows(table0)[:, :, F:2 * F]).then_inc(ld_h, 16)
                sp.wait_ge(zeros_ready, 1)
                for n in range(3):
                    with sp.Fori(0, NB) as i:
                        part = sums[n][ds(i * (TB * P), TB * P), :].rearrange("(p r) c -> p (r c)", p=P)
                        sp.dma_start(part, zeros[:, 0:TB * widths[n]]).then_inc(zeroed, 16)
                sp.wait_ge(zeroed, 16 * 3 * NB)
                for n in range(3):
                    s = passes[n]
                    with sp.Fori(0, NCH) as k:
                        sp.wait_ge(s["g_free"], k + 1)
                        part = lambda a: a[ds(k * P, P)].rearrange("(p a) -> p a", a=1)
                        sp.dma_start(g_src, part(src)).then_inc(s["g_nodes"], 16)
                        sp.dma_start(g_dst, part(dst)).then_inc(s["g_nodes"], 16)
                        sp.dma_start(g_ew, part(ew)).then_inc(s["g_edges"], 16)
                        sp.dma_start(g_row, dst[ds(k * P, P)].partition_broadcast(P)).then_inc(s["g_edges"], 16)
                    sp.wait_ge(pass_done[n], 1)
                    with sp.Fori(0, NB - 1) as k:
                        sums_in(n, k * TB, TB, k)
                        rows_out(n, k * TB, TB, k)
                    sums_in(n, (NB - 1) * TB, TB, NB - 1)
                    last_rows_out(n, (NB - 1) * TB, NB - 1)
                    if n < 2:
                        sp.wait_ge(nodes[n + 1]["row_stored"], 16 * NB)
                        sp.sem_inc(tables_ready[n + 1], 1)
                sp.wait_ge(out_stored, 16 * NB)

        @block.gpsimd
        def _(pool):
            small_ok = dict(allow_small_or_imprecise_dtypes=True)
            pool.iota(iota_row[:, :], pattern=[[1, P]], base=0, channel_multiplier=0, **small_ok).then_inc(iotas, 1)
            pool.iota(iota_col[:, :], pattern=[[0, 1]], base=0, channel_multiplier=1, **small_ok).then_inc(iotas, 1)
            pool.iota(need[:, :], pattern=[[P, EARLY]], base=P, channel_multiplier=0, **small_ok).then_inc(iotas, 1)
            pool.iota(iota_dif[:, :], pattern=[[-1, P]], base=0, channel_multiplier=1, **small_ok).then_inc(iotas, 1)

            s = nodes[0]
            pool.sem_inc(s["pw_made"], 2)

            def split_pair(j):
                for b in range(2):
                    i = 2 * j + b
                    wait_apart(pool, (s["pres_made"], i + 3), (win_stored[b], 16 * j + 16))
                    pool.tensor_copy(pw3[b][:, :, F:2 * F], pres[b][:, :, :]).then_inc(s["pool_own"], 1)
                    wait_apart(pool, (s["pool_own"], i + 1))
                    pool.tensor_tensor(pw3[b][:, :, 2 * F:3 * F], pres[b][:, :, :], pw3[b][:, :, F:2 * F], ALU.subtract)\
                        .then_inc(s["pw_made"], 1)

            with pool.Fori(0, NB // 2) as j:
                split_pair(j)

            windowed = is_windowed(pool)
            for n in range(3):
                s = passes[n]
                width = 2 * F if n == 0 else F
                pool.wait_ge(tables_ready[n], 1)
                with pool.If(windowed):
                    with pool.Fori(0, NIT) as i:
                        for b in range(2):
                            for h in range(U):
                                u = U * b + h
                                wait_apart(pool, (s["idx_ready"][b], (i + 1) * 16), (s["rows_used"][u], i + 1))
                                for j in range(KU):
                                    pool.indirect_dma_start(
                                        out=rows[u][:, j, 0:width], out_offset=None, in_=tables[n],
                                        in_offset=bass.IndirectOffsetOnAxis(ap=idx[b][:, h * KU + j:h * KU + j + 1], axis=0),
                                    ).then_inc(s["rows_ready"][u], 16)
                with pool.Else():
                    with pool.Fori(0, NCH) as k:
                        wait_apart(pool, (s["g_nodes"], (k + 1) * 32))
                        pool.indirect_dma_start(
                            out=g_from[:, 0:width], out_offset=None, in_=tables[n],
                            in_offset=bass.IndirectOffsetOnAxis(ap=g_src, axis=0)).then_inc(s["g_rows"], 16)
                        if n == 0:
                            pool.indirect_dma_start(
                                out=g_to, out_offset=None, in_=tables[n],
                                in_offset=bass.IndirectOffsetOnAxis(ap=g_dst, axis=0)).then_inc(s["g_rows"], 16)
                        pool.indirect_dma_start(
                            out=g_acc[:, 0:widths[n]], out_offset=None, in_=sums[n],
                            in_offset=bass.IndirectOffsetOnAxis(ap=g_dst, axis=0)).then_inc(s["g_sums"], 16)
                        wait_apart(pool, (s["g_new"], k + 1))
                        pool.indirect_dma_start(
                            out=sums[n], out_offset=bass.IndirectOffsetOnAxis(ap=g_put, axis=0),
                            in_=g_new[:, 0:widths[n]], in_offset=None,
                            bounds_check=NP - 1, oob_is_err=False).then_inc(s["g_put"], 16)
                        wait_apart(pool, (s["g_put"], (k + 1) * 16))
                        pool.sem_inc(s["g_free"], 1)
                    pool.sem_inc(pass_done[n], 1)
        @block.scalar
        def _(act):
            act.dma_start(ident[:, :], c["identity"]).then_inc(ident_ready, 16)
            act.dma_start(W14[:, 0:F], c["L0_gnn_W1"]).then_inc(ident_ready, 16)
            act.dma_start(W14[:, F:2 * F], c["L0_gnn_W4"]).then_inc(ident_ready, 16)
            act.dma_start(WG[0][:, :], c["L1_gnn_W1"]).then_inc(ld_const, 16)
            act.dma_start(WG[1][:, :], c["L1_gnn_W2"]).then_inc(ld_const, 16)
            act.dma_start(vec["w2"][:, :], c["L0_gnn_W2"].rearrange("f a -> (f a)").partition_broadcast(P)).then_inc(ld_const, 16)
            act.dma_start(b2col[:, :], c["L0_gnn_b2"].partition_broadcast(P)).then_inc(ld_const, 16)
            for v, name in (("b1", "L0_gnn_b1"), ("b4", "L0_gnn_b4"), ("c1", "L1_gnn_b1"), ("gm1", "L1_gnn_gamma1"),
                            ("bt1", "L1_gnn_beta1"), ("c2", "L1_gnn_b2"), ("gm2", "L1_gnn_gamma2"), ("bt2", "L1_gnn_beta2")):
                act.dma_start(vec[v][:, :], c[name].partition_broadcast(P)).then_inc(ld_const, 16)

            s = nodes[0]
            NH = NB // 2

            def deviations(part):
                lo, hi = XPARTS[part] * TB, XPARTS[part + 1] * TB
                act.wait_ge(stat, part + 1)
                act.activation(rstd[:, lo:hi], rstd[:, lo:hi], ACT.Sqrt).then_inc(sd, 1)
                act.wait_ge(rs, part + 1)

            def relu_a(j, i, b):
                act.wait_ge(s["tr_done"], i + 1)
                act.wait_ge(h_stored[b], 16 * j + 16)
                for t in range(TB):
                    at = ds(i * TB + t, 1)
                    done = act.activation(stage_a[b][:, t, :], tile_of(X, i, t), ACT.Relu, bias=nmr[:, at], scale=rstd[:, at])
                done.then_inc(s["stage_ready"], 1)

            def turned_a(i, b):
                act.wait_ge(s["tr_done"], i + 3)
                act.wait_ge(s["q_mm"], i + 1)
                act.activation(hT_a[b][:, :, :], psT_a[b][:, :, :], ACT.Copy).then_inc(s["hT_ready"], 1)

            def product_a(i, b):
                act.wait_ge(s["q_mm"], i + 3)
                act.activation(blk(Q, i), psQ_a[b], ACT.Copy).then_inc(s["q_out"], 1)

            def pair_a(j, blocks=2, relus=2, turns=2):
                for b in range(blocks):
                    i = 2 * j + b
                    if b < relus:
                        relu_a(j + 1, i + 2, b)
                    if b < turns:
                        turned_a(i + 1, 1 - b)
                    product_a(i, b)

            act.sem_inc(s["q_mm"], 2)
            act.sem_inc(s["tr_done"], 2)
            for b in range(2):
                act.sem_inc(h_stored[b], 16)
            deviations(0)
            relu_a(0, 0, 0)
            relu_a(0, 1, 1)
            turned_a(0, 0)
            pair_a(0)
            deviations(1)
            with act.Fori(1, 3) as j:
                pair_a(j)
            deviations(2)
            with act.Fori(3, NH - 1) as j:
                pair_a(j)
            pair_a(NH - 1, relus=1)
            pair_a(NH, blocks=1, relus=0, turns=0)
            act.wait_ge(ld_const, 16 * 12)

            def deviation(n, t, m, k):
                s = nodes[n + 1]
                act.wait_ge(s["var_ready"], k + 1)
                c = 2 if n == 0 else 1
                act.activation(sdev[:, 0:m, 0:c], var[:, 0:m, 0:c], ACT.Sqrt).then_inc(s["sd_ready"], 1)

            def relu(n, t, m, k):
                s = nodes[n + 1]
                act.wait_ge(s["normed"], k + 2)
                if n == 0:
                    for q in range(m):
                        done = act.activation(stage[:, q, :], tile_at(X, t, q), ACT.Relu, bias=nmrb[:, q:q + 1],
                                              scale=inv[:, q, 0:1])
                else:
                    done = act.activation(stage[:, 0:m, :], gated[:, 0:m, :], ACT.Relu)
                done.then_inc(s["stage_ready"], 1)

            def turned_rows(n, t, m, k):
                s = nodes[n + 1]
                act.wait_ge(s["tr_done"], k + 1)
                act.activation(hT[:, 0:m, :], psT[:, 0:m, :], ACT.Copy).then_inc(s["hT_ready"], 1)

            def act_pass(n, tile_steps):
                s = passes[n]
                w = widths[n]
                for b in range(2):
                    act.sem_inc(s["stored"][b], 16)
                if n == 0:
                    for u in range(2 * U):
                        act.sem_inc(s["rows_used"][u], 1)
                    act.sem_inc(s["sig"], 2)

                def gate_rows(i, b, h):
                    u = U * b + h
                    if h == 0:
                        act.wait_ge(s["acc_done"][b], i + 1)
                        act.wait_ge(s["oh_ready"][b], i + 2)
                    act.wait_ge(s["z_ready"][h], 2 * i + (b + 1))
                    act.activation(V[b][:, h * KU:(h + 1) * KU, C_W:C_W + 1], z[h][:, :].unsqueeze(2),
                                   ACT.Sigmoid, bias=b2col[:, 0:1]).then_inc(s["sig"], 1)
                    act.wait_ge(s["sig"], 4 * i + (2 * b + h + 3))
                    for j in range(KU):
                        jj = h * KU + j
                        done = act.activation(V[b][:, jj, 0:F], rows[u][:, j, F:2 * F], ACT.Copy,
                                              scale=V[b][:, jj, C_W:C_W + 1])
                    done.then_inc(s["rows_used"][u], 1)

                def store_window(i, b):
                    g = 2 * i + b
                    first = first_node(act, g)
                    act.wait_ge(s["acc_done"][b], i + 2)
                    act.wait_ge(s["stored"][b], (i + 1) * 16)
                    act.activation(R[b][:, 0:w], psA[b][:, 0:w], ACT.Copy).then_inc(s["R_ready"][b], 1)
                    act.wait_ge(s["R_ready"][b], i + 2)
                    act.wait_ge(s["stored"][1 - b], (i + (1 + b)) * 16)
                    act.dma_start(sums[n][ds(first, P), :], R[b][:, 0:w]).then_inc(s["stored"][b], 16)

                def pair(i, last, step):
                    if n == 0:
                        gate_rows(i, 1, 0)
                        store_window(i, 0)
                        step(0)
                        gate_rows(i, 1, 1)
                        step(1)
                        if not last:
                            gate_rows(i + 1, 0, 0)
                        store_window(i, 1)
                        step(2)
                        if not last:
                            gate_rows(i + 1, 0, 1)
                        step(3)
                    else:
                        for b in range(2):
                            store_window(i, b)
                            step(2 * b)
                            step(2 * b + 1)

                if n == 0:
                    act.preload_act_table(ACT.Sigmoid)
                    gate_rows(0, 0, 0)
                    gate_rows(0, 0, 1)
                in_quads(act, pair, tile_steps)

            windowed = is_windowed(act)
            with act.If(windowed):
                for n in range(3):
                    steps = ({0: deviation, 2: relu, 4: turned_rows}, {0: deviation, 1: relu, 2: turned_rows}, {0: deviation})[n]
                    act_pass(n, {at: partial(step, n) for at, step in steps.items()})
                    for call in ((EARLY, LATE, EARLY), (LAST, 1, EARLY + 1)):
                        for step in steps.values():
                            step(n, *call)
                for b in range(2):
                    act.wait_ge(passes[2]["stored"][b], 16 * (NIT + 1))
            with act.Else():
                for n in range(3):
                    s = passes[n]
                    if n == 0:
                        with act.Fori(0, NCH) as k:
                            act.wait_ge(s["g_z"], k + 1)
                            act.activation(g_v[:, C_W:C_W + 1], g_z, ACT.Sigmoid, bias=b2col[:, 0:1]).then_inc(s["g_w"], 1)
                    with act.Fori(0, NB) as k:
                        deviation(n, k * TB, TB, k)
                        if n < 2:
                            relu(n, k * TB, TB, k)
                            turned_rows(n, k * TB, TB, k)

        @block.tensor
        def _(pe):
            pe.wait_ge(ident_ready, 48)
            s = nodes[0]

            def turn_a(i, b):
                pe.wait_ge(s["stage_ready"], i + 1)
                pe.wait_ge(s["hT_ready"], i + 1)
                for t in range(TB):
                    done = pe.transpose(psT_a[b][:, t, :], stage_a[b][:, t, :], ident[:, :])
                done.then_inc(s["tr_done"], 1)

            def products_a(i, b):
                pe.wait_ge(s["hT_ready"], i + 3)
                pe.wait_ge(s["pres_made"], i + 1)
                for t in range(TB):
                    done = pe.matmul(psP_a[b][:, t, :], hT_a[b][:, t, :], W14[:, 0:F], start=True, stop=True)
                done.then_inc(s["p_mm"], 1)
                pe.wait_ge(s["q_out"], i + 1)
                for t in range(TB):
                    done = pe.matmul(psQ_a[b][:, t, :], hT_a[b][:, t, :], W14[:, F:2 * F], start=True, stop=True)
                done.then_inc(s["q_mm"], 1)

            for name in ("hT_ready", "pres_made", "q_out"):
                pe.sem_inc(s[name], 2)
            turn_a(0, 0)
            with pe.Fori(0, NB // 2) as j:
                for b in range(2):
                    turn_a(2 * j + b + 1, 1 - b)
                    products_a(2 * j + b, b)
            products_a(NB - 1, 0)
            pe.wait_ge(ld_const, 16 * 12)
            pe.wait_ge(s["pres_made"], NB + 2)
            pe.wait_ge(s["q_out"], NB + 2)

            def turn(n, t, m, k):
                s = nodes[n + 1]
                pe.wait_ge(s["stage_ready"], k + 1)
                for q in range(m):
                    done = pe.transpose(psT[:, q, :], stage[:, q, :], ident[:, :])
                done.then_inc(s["tr_done"], 1)

            def product(n, t, m, k):
                s = nodes[n + 1]
                pe.wait_ge(s["hT_ready"], k + 1)
                pe.wait_ge(s["out_done"], k + 1)
                for q in range(m):
                    done = pe.matmul(psO[:, q, 0:F], hT[:, q, :], WG[n][:, :], start=True, stop=True)
                done.then_inc(s["mm_done"], 1)

            def pe_pass(n, tile_steps):
                s = passes[n]
                w = widths[n]
                for b in range(2):
                    pe.sem_inc(s["acc_done"][b], 1)
                if n:
                    for u in range(2 * U):
                        pe.sem_inc(s["rows_used"][u], 1)

                def at_dst(i, b, h, back):
                    i = i + back
                    pe.wait_ge(s["ohT_ready"][b], i + 1)
                    pe.wait_ge(s["pwin_ready"][b], (i + 1) * 16)
                    pe.wait_ge(s["psE_free"][h], 2 * i + (b + 1))
                    for j in range(KU):
                        for part in range(3):
                            done = pe.matmul(psE[h][:, j, :], ohT[b][:, h * KU + j, :],
                                             pwin[b][:, part * F:(part + 1) * F],
                                             start=(part == 0), stop=(part == 2))
                    done.then_inc(s["psE_ready"][h], 1)

                def sum_unit(i, b, h):
                    u = U * b + h
                    if n == 0:
                        pe.wait_ge(s["rows_used"][u], i + 2)
                    else:
                        pe.wait_ge(s["rows_ready"][u], (i + 1) * 16 * KU)
                    for j in range(KU):
                        jj = h * KU + j
                        value = V[b][:, jj, 0:w] if n == 0 else rows[u][:, j, 0:F]
                        done = pe.matmul(psA[b][:, 0:w], oh[b][:, jj, :], value, start=(jj == 0), stop=False)
                    if n:
                        done.then_inc(s["rows_used"][u], 1)

                def pair(i, last, step):
                    for b in range(2):
                        for h in range(U):
                            if n == 0:
                                at_dst(i, 1 - b, h, b)
                            if h == 0:
                                pe.wait_ge(s["oh_ready"][b], i + 2)
                                pe.wait_ge(s["R_ready"][b], i + 1)
                            sum_unit(i, b, h)
                            if h == 0:
                                step(2 * b)
                        pe.wait_ge(s["R_ready"][1 - b], i + 1 + b)
                        pe.matmul(psA[b][:, 0:w], shift[b][:, :], R[1 - b][:, 0:w], start=False, stop=True)\
                          .then_inc(s["acc_done"][b], 1)
                        step(2 * b + 1)

                if n == 0:
                    for h in range(U):
                        at_dst(0, 0, h, 0)
                in_quads(pe, pair, tile_steps)

            windowed = is_windowed(pe)
            with pe.If(windowed):
                for n in range(3):
                    steps = ({5: turn, 6: product}, {2: turn, 4: product}, {})[n]
                    pe_pass(n, {at: partial(step, n) for at, step in steps.items()})
                    for call in ((EARLY, LATE, EARLY), (LAST, 1, EARLY + 1)):
                        for step in steps.values():
                            step(n, *call)
            with pe.Else():
                for n in range(3):
                    s = passes[n]
                    w = widths[n]
                    with pe.Fori(0, NCH) as k:
                        pe.wait_ge(s["g_v"], k + 1)
                        pe.matmul(psA[0][:, 0:w], g_eq, g_v[:, 0:w], start=True, stop=True).then_inc(s["g_mm"], 1)
                    if n < 2:
                        with pe.Fori(0, NB) as k:
                            turn(n, k * TB, TB, k)
                            product(n, k * TB, TB, k)

        @block.vector
        def _(dve):
            for b in range(2):
                dve.memset(V[b][:, :, C_ONE:C_ONE + 1], 1.0)
            dve.wait_ge(iotas, 4)
            dve.tensor_scalar(below[:, :], iota_dif[:, :], 0.0, None, ALU.is_gt)

            s = nodes[0]

            def statistics(part):
                lo, hi = XPARTS[part], XPARTS[part + 1]
                dve.wait_ge(ld_x[part], 16)
                for t in range(lo * TB, hi * TB):
                    done = dve.bn_stats(stats_x[:, t, :], X[:, t, :])
                done.then_inc(s["own"], 1)
                dve.wait_ge(s["own"], 2 * part + 1)
                for t in range(lo * TB, hi * TB):
                    done = dve.bn_aggr(mv[:, t, :], stats_x[:, t, :])
                done.then_inc(s["own"], 1)
                dve.wait_ge(s["own"], 2 * part + 2)
                at = slice(lo * TB, hi * TB)
                dve.tensor_scalar(rstd[:, at].unsqueeze(2), mv[:, at, 1:2], EPS, None, ALU.add).then_inc(stat, 1)
                dve.wait_ge(sd, part + 1)
                dve.reciprocal(rstd[:, at], rstd[:, at]).then_inc(norm, 1)
                dve.wait_ge(norm, part + 1)
                dve.scalar_tensor_tensor(nmr[:, at].unsqueeze(2), mv[:, at, 0:1], -1.0, rstd[:, at].unsqueeze(2),
                                         ALU.mult, ALU.mult).then_inc(rs, 1)

            def rows_pair(j, blocks=2):
                for b in range(blocks):
                    i = 2 * j + b
                    dve.wait_ge(s["p_mm"], i + 1)
                    dve.wait_ge(p_stored[b], 16 * j + 16)
                    dve.tensor_tensor(tst[b][:, :, :], psP_a[b], per_feature(vec["b1"]), ALU.subtract).then_inc(s["p_made"], 1)
                    dve.wait_ge(win_stored[b], 16 * j + 16)
                    dve.tensor_copy(pw3[b][:, :, 0:F], psP_a[b]).then_inc(s["pw1_made"], 1)
                    dve.wait_ge(s["pw1_made"], i + 1)
                    dve.wait_ge(s["pw_made"], i + 1)
                    dve.tensor_tensor(pres[b][:, :, :], psP_a[b], pw3[b][:, :, 0:F], ALU.subtract).then_inc(s["pres_made"], 1)

            for b in range(2):
                dve.sem_inc(p_stored[b], 16)
                dve.sem_inc(win_stored[b], 16)
            statistics(0)
            dve.wait_ge(ld_const, 16 * 12)
            rows_pair(0)
            statistics(1)
            rows_pair(1)
            statistics(2)
            rows_pair(2)
            dve.wait_ge(ld_edge, 32)
            dve.tensor_copy(basef[:, :].unsqueeze(2), by_group(dst_i)[:, :, 0:1]).then_inc(pro, 1)
            dve.tensor_tensor(gap, nxt_i, dst_i, ALU.subtract).then_inc(pro, 1)
            dve.wait_ge(pro, 1)
            dve.tensor_tensor(span[:, :].unsqueeze(2), by_group(dst_i)[:, :, GE - 1:GE], basef[:, :].unsqueeze(2),
                              ALU.subtract).then_inc(pro, 1)
            dve.wait_ge(pro, 3)
            dve.tensor_reduce(small[:, 0:1], gap, AX.X, ALU.min).then_inc(pro, 1)
            dve.tensor_reduce(small[:, 1:2], span[:, :], AX.X, ALU.max).then_inc(pro, 1)
            dve.wait_ge(pro, 5)
            dve.tensor_scalar(small[:, 2:3], small[:, 1:2], -1.0, float(P - 1), ALU.mult, ALU.add).then_inc(pro, 1)
            dve.wait_ge(pro, 6)
            dve.tensor_tensor(fits[:, :], small[:, 2:3], small[:, 0:1], ALU.min).then_inc(base_ready, 1)
            rows_pair(3)
            for q in range(GPP):
                dve.tensor_scalar(by_group(relp_all)[:, q, :], by_group(dst_i)[:, q, :], basef[:, q:q + 1], None,
                                  ALU.subtract)
                done = dve.tensor_scalar(by_group(relr_all)[:, q, :].rearrange("r (j p) -> r p j", j=K),
                                         by_group(dst_i)[:, q, :].rearrange("r (p j) -> r p j", j=K),
                                         basef[:, q:q + 1], None, ALU.subtract)
            done.then_inc(rel_made, 1)
            rows_pair(4)
            dve.memset(delta[:, 0:1], 0.0)
            dve.wait_ge(base_back, 32)
            dve.tensor_tensor(delta[:, 1:NGP], base_all[:, 1:NGP], base_all[:, 0:NGP - 1], ALU.subtract).then_inc(pro, 1)
            dve.tensor_copy(first_i[:, :], base_all[0:1, :])
            at = GROWS
            dve.tensor_tensor(slack[:, at:at + EARLY], base_all[0:1, 4 * (LAG - 1):4 * (QUADS - 1):4], need[:, :], ALU.subtract)
            at += EARLY
            dve.wait_ge(pro, 7)
            dve.tensor_scalar(slack[:, at:at + NG - 1], delta[0:1, 1:NG], -1.0, float(P), ALU.mult, ALU.add)
            at += NG - 1
            dve.tensor_scalar(slack[:, at:at + 1], base_all[0:1, 0:1], -1.0, None, ALU.mult)
            dve.tensor_scalar(slack[:, at + 1:at + 2], base_all[0:1, NG - 2:NG - 1], float(LAST * P), None,
                              ALU.subtract).then_inc(pro, 1)
            dve.wait_ge(pro, 8)
            dve.tensor_reduce(worst[:, :], slack, AX.X, ALU.min).then_inc(pro, 1)
            dve.wait_ge(pro, 9)
            dve.tensor_scalar(flag[:, :], worst[:, :], 0.0, None, ALU.is_ge).then_inc(flag_ready, 1)
            rows_pair(5)
            rows_pair(NB // 2, 1)
            dve.wait_ge(s["pres_made"], NB + 2)
            dve.tensor_copy(pw3[0][:, :, F:2 * F], pres[0][:, :, :]).then_inc(s["own"], 1)
            dve.wait_ge(s["own"], 2 * (len(XPARTS) - 1) + 1)
            dve.tensor_tensor(pw3[0][:, :, 2 * F:3 * F], pres[0][:, :, :], pw3[0][:, :, F:2 * F], ALU.subtract)\
               .then_inc(s["last_pw_made"], 1)

            def node_sums(n, t, m, k):
                s = nodes[n + 1]
                own = lambda step: (s["own"], k * OWN_STEPS[n] + step)
                these = ds(t, m)
                dve.wait_ge(s["sums_back"], 16 * k + 16)
                dve.wait_ge(s["normed"], k + 1)
                if n == 0:
                    dve.wait_ge(ld_h, 16)
                    dve.tensor_tensor(Q[:, these, :], Q[:, these, :], vec["b4"][:, :].unsqueeze(1).broadcast_to([P, m, F]),
                                      ALU.add).then_inc(s["own"], 1)
                    dve.wait_ge(*own(1))
                    for q in range(m):
                        sum_w, count = (A[:, ds(t + q, 1), c:c + 1].rearrange("p a f -> p (a f)") for c in (C_W, C_ONE))
                        dve.scalar_tensor_tensor(tile_at(H, t, q), tile_at(H, t, q), sum_w, tile_at(A, t, q),
                                                 ALU.mult, ALU.subtract)
                        done = dve.scalar_tensor_tensor(tile_at(Q, t, q), tile_at(Q, t, q), count, tile_at(X, t, q),
                                                        ALU.mult, ALU.add)
                    done.then_inc(s["own"], 1)
                    dve.wait_ge(*own(2))
                    dve.tensor_tensor(X[:, these, :], H[:, these, :], Q[:, these, :], ALU.add).then_inc(s["own"], 1)
                    into = X
                else:
                    dve.tensor_tensor(A[:, these, 0:F], A[:, these, 0:F], G[:, these, :], ALU.add).then_inc(s["own"], 1)
                    dve.wait_ge(*own(1))
                    for q in range(m):
                        done = dve.scalar_tensor_tensor(tile_at(H, t, q), tile_at(A, t, q), dinv[:, ds(t + q, 1)],
                                                        vec[f"c{n}"][:, :], ALU.mult, ALU.add)
                    done.then_inc(s["own"], 1)
                    into = H
                z = 1 if n == 0 else 0
                wait_apart(dve, own(2 + z))
                for q in range(m):
                    done = dve.bn_stats(stats[:, q, :], tile_at(into, t, q))
                done.then_inc(s["own"], 1)
                wait_apart(dve, own(3 + z))
                for q in range(m):
                    done = dve.bn_aggr(mvb[:, q, :], stats[:, q, :])
                done.then_inc(s["own"], 1)
                dve.wait_ge(*own(4 + z))
                if n == 0:
                    dve.tensor_scalar(var[:, 0:m, 1:2], A[:, these, C_EW:C_EW + 1], 1.0, None, ALU.add)
                dve.tensor_scalar(var[:, 0:m, 0:1], mvb[:, 0:m, 1:2], EPS, None, ALU.add).then_inc(s["var_ready"], 1)

            def node_norm(n, t, m, k):
                s = nodes[n + 1]
                own = lambda step: (s["own"], k * OWN_STEPS[n] + step)
                c = 2 if n == 0 else 1
                dve.wait_ge(s["sd_ready"], k + 1)
                dve.reciprocal(inv[:, 0:m, 0:c], sdev[:, 0:m, 0:c]).then_inc(s["own"], 1)
                dve.wait_ge(*own(6 if n == 0 else 5))
                if n == 0:
                    dve.tensor_copy(dinv[:, ds(t, m)].unsqueeze(2), inv[:, 0:m, 1:2])
                    dve.scalar_tensor_tensor(nmrb[:, 0:m].unsqueeze(2), mvb[:, 0:m, 0:1], -1.0, inv[:, 0:m, 0:1],
                                             ALU.mult, ALU.mult).then_inc(s["normed"], 1)
                    return
                for q in range(m):
                    done = dve.scalar_tensor_tensor(diff[:, q, :], tile_at(H, t, q), mvb[:, q, 0:1], vec[f"gm{n}"][:, :],
                                                    ALU.subtract, ALU.mult)
                done.then_inc(s["own"], 1)
                dve.wait_ge(*own(6))
                for q in range(m):
                    done = dve.scalar_tensor_tensor(gated[:, q, :], diff[:, q, :], inv[:, q, 0:1], vec[f"bt{n}"][:, :],
                                                    ALU.mult, ALU.add)
                if n == 1:
                    done.then_inc(s["normed"], 1)
                else:
                    done.then_inc(s["own"], 1)
                    dve.wait_ge(*own(7))
                    dve.tensor_tensor(H[:, ds(t, m), :], gated[:, 0:m, :], X[:, ds(t, m), :], ALU.add).then_inc(s["normed"], 1)

            def node_scale(n, t, m, k):
                s = nodes[n + 1]
                dve.wait_ge(s["mm_done"], k + 1)
                dve.tensor_tensor(G[:, ds(t, m), :], psO[:, 0:m, 0:F],
                                  dinv[:, ds(t, m)].unsqueeze(2).broadcast_to([P, m, F]), ALU.mult).then_inc(s["out_done"], 1)

            for n in range(3):
                dve.sem_inc(nodes[n + 1]["normed"], 1)
                if n < 2:
                    dve.sem_inc(nodes[n + 1]["out_done"], 1)

            def dve_pass(n, tile_steps):
                s = passes[n]
                dve.memset(R[1][:, :], 0.0).then_inc(s["R_ready"][1], 1)
                dve.sem_inc(s["R_ready"][0], 1)
                for b in range(2):
                    dve.sem_inc(s["oh_ready"][b], 1)
                    if n == 0:
                        dve.sem_inc(s["psE_free"][b], 1)

                def one_hot_rows(i, b, back):
                    i = i + back
                    dve.wait_ge(s["rel_ready"][b], (i + 1) * 48)
                    dve.tensor_scalar(ohT[b][:, :, :], relr[b][:, :].rearrange("p (j e) -> p j e", j=K),
                                      iota_col[:, 0:1], None, ALU.is_equal).then_inc(s["ohT_ready"][b], 1)

                def one_hots(i, b, back):
                    i = i + back
                    g = 2 * i + b
                    if n:
                        dve.wait_ge(s["rel_ready"][b], (i + 1) * 32)
                    dve.wait_ge(s["acc_done"][b], i + 1)
                    node = iota_row[:, :].unsqueeze(1).broadcast_to([P, K, P])
                    rel = relp[b][:, :].unsqueeze(2).broadcast_to([P, K, P])
                    dve.tensor_scalar(shift[b][:, :], iota_dif[:, :], delta[:, ds(g, 1)], None, ALU.is_equal)
                    if n == 0:
                        dve.tensor_copy(V[b][:, :, C_EW:C_EW + 1], eww[b][:, :].unsqueeze(2))
                        dve.tensor_tensor(oh[b][:, :, :], node, rel, ALU.is_equal).then_inc(s["oh_ready"][b], 1)
                    else:
                        dve.wait_ge(s["oh_ready"][1 - b], i + (1 + b))
                        dve.tensor_tensor(eqm[:, :, :], node, rel, ALU.is_equal).then_inc(s["eq"][b], 1)
                        dve.wait_ge(s["eq"][b], i + 1)
                        dve.tensor_tensor(oh[b][:, :, :], eqm[:, :, :], eww[b][:, :].unsqueeze(2).broadcast_to([P, K, P]),
                                          ALU.mult).then_inc(s["oh_ready"][b], 1)

                def gate_sums(i, b, h):
                    u = U * b + h
                    dve.wait_ge(s["psE_ready"][h], 2 * i + (b + 1))
                    dve.wait_ge(s["rows_ready"][u], (i + 1) * 16 * KU)
                    dve.tensor_tensor(diff[:, :, :], psE[h][:, :, :], rows[u][:, :, 0:F], ALU.subtract)\
                       .then_inc(s["psE_free"][h], 1)
                    dve.wait_ge(s["psE_free"][h], 2 * i + (b + 2))
                    dve.scalar_tensor_tensor(gated[:, :, :], diff[:, :, :], 0.0, per_feature(vec["w2"]),
                                             ALU.max, ALU.mult).then_inc(s["gated"], 1)
                    dve.wait_ge(s["gated"], 4 * i + (2 * b + h + 1))
                    dve.wait_ge(s["sig"], 4 * i + (2 * b + h + 1))
                    dve.tensor_reduce(z[h][:, :], gated[:, :, :], AX.X, ALU.add).then_inc(s["z_ready"][h], 1)

                def pair(i, last, step):
                    for b in range(2):
                        if n == 0:
                            one_hot_rows(i, 1 - b, b)
                            gate_sums(i, b, 0)
                            step(2 * b)
                            one_hots(i, 1 - b, b)
                            gate_sums(i, b, 1)
                            step(2 * b + 1)
                        else:
                            one_hots(i, b, 0)
                            step(2 * b)
                            step(2 * b + 1)

                if n == 0:
                    one_hot_rows(0, 0, 0)
                    one_hots(0, 0, 0)
                in_quads(dve, pair, tile_steps)

            windowed = is_windowed(dve)
            with dve.If(windowed):
                for n in range(3):
                    steps = ({0: node_sums, 3: node_norm, 7: node_scale}, {0: node_sums, 3: node_norm, 6: node_scale},
                             {0: node_sums, 3: node_norm})[n]
                    dve_pass(n, {at: partial(step, n) for at, step in steps.items()})
                    others, last = (EARLY, LATE, EARLY), (LAST, 1, EARLY + 1)
                    node_sums(n, *others)
                    node_norm(n, *others)
                    node_sums(n, *last)
                    if n < 2:
                        node_scale(n, *others)
                    node_norm(n, *last)
                    if n < 2:
                        node_scale(n, *last)
            with dve.Else():
                dve.wait_ge(tables_ready[0], 1)
                dve.memset(zeros, 0.0).then_inc(zeros_ready, 1)
                for n in range(3):
                    s = passes[n]
                    w = widths[n]
                    OWN = 8 if n == 0 else 4
                    gathers = 2 if n == 0 else 1
                    dve.sem_inc(s["g_free"], 1)
                    with dve.Fori(0, NCH) as k:
                        own = lambda m: dve.wait_ge(s["g_own"], k * OWN + m)
                        dve.wait_ge(s["g_nodes"], (k + 1) * 32)
                        dve.wait_ge(s["g_edges"], (k + 1) * 32)
                        dve.tensor_copy(g_dstf, g_dst).then_inc(s["g_own"], 1)
                        own(1)
                        dve.tensor_scalar(g_eq, g_row, g_dstf, None, ALU.is_equal).then_inc(s["g_own"], 1)
                        own(2)
                        dve.tensor_tensor(g_low, g_eq, below[:, :], ALU.mult).then_inc(s["g_own"], 1)
                        own(3)
                        dve.tensor_reduce(g_cnt, g_low, AX.X, ALU.max).then_inc(s["g_own"], 1)
                        own(4)
                        dve.scalar_tensor_tensor(g_put, g_cnt, float(2 * NP), g_dstf, ALU.mult, ALU.add)
                        dve.wait_ge(s["g_rows"], (k + 1) * (16 * gathers))
                        if n == 0:
                            dve.tensor_tensor(diff[:, 0, :], g_to[:, 0:F], g_from[:, 0:F], ALU.subtract).then_inc(s["g_own"], 1)
                            own(5)
                            dve.tensor_tensor(diff[:, 1, :], diff[:, 0, :], vec["b1"][:, :], ALU.add).then_inc(s["g_own"], 1)
                            own(6)
                            dve.scalar_tensor_tensor(gated[:, 0, :], diff[:, 1, :], 0.0, vec["w2"][:, :], ALU.max, ALU.mult)\
                               .then_inc(s["g_own"], 1)
                            own(7)
                            dve.tensor_reduce(g_z, gated[:, 0, :], AX.X, ALU.add).then_inc(s["g_z"], 1)
                            dve.tensor_copy(g_v[:, C_EW:C_EW + 1], g_ew).then_inc(s["g_own"], 1)
                            dve.wait_ge(s["g_w"], k + 1)
                            own(8)
                            dve.tensor_scalar(g_v[:, 0:F], g_from[:, F:2 * F], g_v[:, C_W:C_W + 1], None, ALU.mult)\
                               .then_inc(s["g_v"], 1)
                        else:
                            dve.tensor_scalar(g_v[:, 0:F], g_from[:, 0:F], g_ew, None, ALU.mult).then_inc(s["g_v"], 1)
                        dve.wait_ge(s["g_mm"], k + 1)
                        dve.wait_ge(s["g_sums"], (k + 1) * 16)
                        dve.tensor_tensor(g_new[:, 0:w], psA[0][:, 0:w], g_acc[:, 0:w], ALU.add).then_inc(s["g_new"], 1)

                    with dve.Fori(0, NB) as k:
                        node_sums(n, k * TB, TB, k)
                        node_norm(n, k * TB, TB, k)
                        if n < 2:
                            node_scale(n, k * TB, TB, k)


_WEIGHTS = ["L0_gnn_W1", "L0_gnn_b1", "L0_gnn_W2", "L0_gnn_b2", "L0_gnn_W4", "L0_gnn_b4", "L1_gnn_W1", "L1_gnn_b1",
            "L1_gnn_gamma1", "L1_gnn_beta1", "L1_gnn_W2", "L1_gnn_b2", "L1_gnn_gamma2", "L1_gnn_beta2"]


def kernel(**inputs):
    import numpy as np
    import concourse.bacc as bacc
    from concourse.bass_utils import run_bass_kernel_spmd

    def padded(a, n, value):
        out = np.full((n,) + a.shape[1:], value, a.dtype)
        out[:a.shape[0]] = a
        return out

    arrays = {
        "x": padded(np.asarray(inputs["x"]), NP, 0),
        "src": padded(np.asarray(inputs["src"]), EP, 0),
        "dst": padded(np.asarray(inputs["dst"]), EP + 1, N),
        "edge_weight": padded(np.asarray(inputs["edge_weight"]), EP, 0),
        "identity": np.eye(P, dtype=np.float32),
    }
    for name in _WEIGHTS:
        arrays[name] = np.ascontiguousarray(inputs[name])

    nc = bacc.Bacc("TRN2", target_bir_lowering=False, num_devices=1)
    args = {}
    for name, a in arrays.items():
        args[name] = nc.dram_tensor(f"in_{name}", a.shape, mybir.dt.from_np(a.dtype), kind="ExternalInput").ap()
    out = nc.dram_tensor("out_x", (N, F), F32, kind="ExternalOutput").ap()
    build_program(nc, args["x"], args["src"], args["dst"], args["edge_weight"], args, out)
    r = run_bass_kernel_spmd(nc, [{f"in_{k}": v for k, v in arrays.items()}], core_ids=[0])
    return r.results[0]["out_x"]
```
